# Optimizing a Trainium2 kernel written in Bass

```python
import numpy as np
import jax
import jax.numpy as jnp

def _softmax(x, axis=-1):
    return jax.nn.softmax(x, axis=axis)
def _gelu(x):
    return jax.nn.gelu(x, approximate=True)
def _silu(x):
    return jax.nn.silu(x)
def _sigmoid(x):
    return jax.nn.sigmoid(x)
def _layernorm(x, axis=-1, eps=1e-5):
    m = jnp.mean(x, axis=axis, keepdims=True)
    v = jnp.var(x, axis=axis, keepdims=True)
    return (x - m) / jnp.sqrt(v + eps)
def _scatter_add(tgt, idx, src, axis=0):
    return tgt.at[idx].add(src)
def _segment_sum(src, seg, n):
    return jax.ops.segment_sum(src, seg, n)

kernel_name = 'mk_conv_preact_d2_conv_nchw192_122339'

def setup_inputs(seed: int = 0):
    np.random.seed(seed)
    _w = jnp.asarray
    def _rec_inputs():
        import jax
        import jax.numpy as jnp
        _gk = jax.random.key(seed)
        x = -0.001003 + 1 * jax.random.normal(jax.random.fold_in(_gk, 1), (2, 192, 64, 64), jnp.float32)
        return x
    x = _rec_inputs()
    def _L0_conv_setup():
        import jax, jax.numpy as jnp
        import numpy as np
        from jax import lax
        DIM = 192
        HEADS = 4
        EPS = 1e-12

        def _l2norm(t, axis):
            n = jnp.sqrt(jnp.sum(t * t, axis=axis, keepdims=True))
            return t / jnp.maximum(n, EPS)
        key = jax.random.key(seed)
        ks = jax.random.split(key, 8)
        b, c, h, w = (2, DIM, 64, 64)
        x = jax.random.normal(ks[0], (b, c, h, w), dtype=jnp.float32)
        w_qkv = jax.random.normal(ks[1], (3 * c, c), dtype=jnp.float32) * 0.05
        b_qkv = jax.random.normal(ks[2], (3 * c,), dtype=jnp.float32) * 0.05
        w_dw = jax.random.normal(ks[3], (3 * c, 1, 3, 3), dtype=jnp.float32) * 0.05
        b_dw = jax.random.normal(ks[4], (3 * c,), dtype=jnp.float32) * 0.05
        w_proj = jax.random.normal(ks[5], (c, c), dtype=jnp.float32) * 0.05
        b_proj = jax.random.normal(ks[6], (c,), dtype=jnp.float32) * 0.05
        temperature = jnp.ones((HEADS, 1, 1), dtype=jnp.float32)
        return {'x': x, 'w_qkv': w_qkv, 'b_qkv': b_qkv, 'w_dw': w_dw, 'b_dw': b_dw, 'w_proj': w_proj, 'b_proj': b_proj, 'temperature': temperature}
    _L0_conv_all = _L0_conv_setup()
    _L0_conv_in = {k: v for k, v in _L0_conv_all.items() if k in ('w_qkv', 'b_qkv', 'w_dw', 'b_dw', 'w_proj', 'b_proj', 'temperature', )}
    del _L0_conv_all

    def _L1_conv_setup():
        import jax, jax.numpy as jnp
        import numpy as np
        B, C, H, W = (16, 192, 48, 48)
        EPS = 1e-05
        key = jax.random.key(seed)
        ks = jax.random.split(key, 5)
        dim = C
        x = jax.random.normal(ks[0], (B, C, H, W), dtype=jnp.float32)
        ln_w = jnp.ones((dim,), dtype=jnp.float32)
        ln_b = jnp.zeros((dim,), dtype=jnp.float32)
        s = 1.0 / np.sqrt(dim)
        Wq = jax.random.uniform(ks[1], (dim, dim), jnp.float32, -s, s)
        Wk = jax.random.uniform(ks[2], (dim, dim), jnp.float32, -s, s)
        Wv = jax.random.uniform(ks[3], (dim, dim), jnp.float32, -s, s)
        w1 = jnp.ones((1,), dtype=jnp.float32)
        w2 = jnp.ones((1,), dtype=jnp.float32)
        return {'x': x, 'ln_w': ln_w, 'ln_b': ln_b, 'Wq': Wq, 'Wk': Wk, 'Wv': Wv, 'w1': w1, 'w2': w2}
    _L1_conv_all = _L1_conv_setup()
    _L1_conv_in = {k: v for k, v in _L1_conv_all.items() if k in ('ln_w', 'ln_b', 'Wq', 'Wk', 'Wv', 'w1', 'w2', )}
    del _L1_conv_all

    return {
        "x": x,
        "L0_conv_w_qkv": _L0_conv_in["w_qkv"],
        "L0_conv_b_qkv": _L0_conv_in["b_qkv"],
        "L0_conv_w_dw": _L0_conv_in["w_dw"],
        "L0_conv_b_dw": _L0_conv_in["b_dw"],
        "L0_conv_w_proj": _L0_conv_in["w_proj"],
        "L0_conv_b_proj": _L0_conv_in["b_proj"],
        "L0_conv_temperature": _L0_conv_in["temperature"],
        "L1_conv_ln_w": _L1_conv_in["ln_w"],
        "L1_conv_ln_b": _L1_conv_in["ln_b"],
        "L1_conv_Wq": _L1_conv_in["Wq"],
        "L1_conv_Wk": _L1_conv_in["Wk"],
        "L1_conv_Wv": _L1_conv_in["Wv"],
        "L1_conv_w1": _L1_conv_in["w1"],
        "L1_conv_w2": _L1_conv_in["w2"],
    }

def reference(x, L0_conv_w_qkv, L0_conv_b_qkv, L0_conv_w_dw, L0_conv_b_dw, L0_conv_w_proj, L0_conv_b_proj, L0_conv_temperature, L1_conv_ln_w, L1_conv_ln_b, L1_conv_Wq, L1_conv_Wk, L1_conv_Wv, L1_conv_w1, L1_conv_w2):
    import jax
    import jax.numpy as jnp
    def _L0_conv_ref(x, w_qkv, b_qkv, w_dw, b_dw, w_proj, b_proj, temperature):
        import jax, jax.numpy as jnp
        import numpy as np
        from jax import lax
        DIM = 192
        HEADS = 4
        EPS = 1e-12

        def _l2norm(t, axis):
            n = jnp.sqrt(jnp.sum(t * t, axis=axis, keepdims=True))
            return t / jnp.maximum(n, EPS)
        b, c, h, w = x.shape
        heads = temperature.shape[0]
        hd = c // heads
        qkv = jnp.einsum('bchw,oc->bohw', x, w_qkv) + b_qkv[None, :, None, None]
        qkv = lax.conv_general_dilated(qkv, w_dw, window_strides=(1, 1), padding=((1, 1), (1, 1)), dimension_numbers=('NCHW', 'OIHW', 'NCHW'), feature_group_count=3 * c) + b_dw[None, :, None, None]
        q, k, v = jnp.split(qkv, 3, axis=1)
        q = q.reshape(b, heads, hd, h * w)
        k = k.reshape(b, heads, hd, h * w)
        v = v.reshape(b, heads, hd, h * w)
        q = _l2norm(q, axis=2)
        k = _l2norm(k, axis=2)
        attn = jnp.einsum('bhdn,bhdm->bhnm', q, k) * temperature[None]
        attn = jax.nn.softmax(attn, axis=-1)
        out = jnp.einsum('bhnm,bhdm->bhdn', attn, v)
        out = out.reshape(b, c, h, w)
        out = jnp.einsum('bchw,oc->bohw', out, w_proj) + b_proj[None, :, None, None]
        return out

    def _L1_conv_ref(x, ln_w, ln_b, Wq, Wk, Wv, w1, w2):
        import jax, jax.numpy as jnp
        import numpy as np
        B, C, H, W = (16, 192, 48, 48)
        EPS = 1e-05
        b, c, h, w = x.shape
        xf = x.reshape(b, c, h * w).transpose(0, 2, 1)
        mu = jnp.mean(xf, axis=-1, keepdims=True)
        var = jnp.mean(jnp.square(xf - mu), axis=-1, keepdims=True)
        xn = (xf - mu) * jax.lax.rsqrt(var + EPS) * ln_w + ln_b
        Q = jnp.einsum('bnc,dc->bnd', xn, Wq)
        K = jnp.einsum('bnc,dc->bnd', xn, Wk)
        V = jnp.einsum('bnc,dc->bnd', xn, Wv)
        S = jnp.einsum('bnd,bmd->bnm', Q, K)
        attn1 = jax.nn.softmax(S, axis=-1)
        attn2 = jnp.square(jax.nn.relu(S))
        e1, e2 = (jnp.exp(w1), jnp.exp(w2))
        denom = e1 + e2
        attn = e1 / denom * attn1 + e2 / denom * attn2
        out = jnp.einsum('bnm,bmd->bnd', attn, V)
        out = out.transpose(0, 2, 1).reshape(b, c, h, w)
        return out + x

    def _gn(v, G=32, eps=1e-5):
        B_, C_, H_, W_ = v.shape
        g = v.reshape(B_, G, C_ // G, H_, W_)
        m = jnp.mean(g, axis=(2, 3, 4), keepdims=True)
        s = jnp.var(g, axis=(2, 3, 4), keepdims=True)
        return ((g - m) / jnp.sqrt(s + eps)).reshape(v.shape)

    def _ln_c(v, eps=1e-6):
        m = jnp.mean(v, axis=1, keepdims=True)
        s = jnp.var(v, axis=1, keepdims=True)
        return (v - m) / jnp.sqrt(s + eps)

    def _ln_t(v, eps=1e-5):
        m = jnp.mean(v, axis=-1, keepdims=True)
        s = jnp.var(v, axis=-1, keepdims=True)
        return (v - m) / jnp.sqrt(s + eps)

    def _to_tokens(v):
        B_, C_, H_, W_ = v.shape
        return v.reshape(B_, C_, H_ * W_).transpose(0, 2, 1)
    def _from_tokens(t, like):
        B_, C_, H_, W_ = like.shape
        return t.transpose(0, 2, 1).reshape(B_, C_, H_, W_)

    x = x + _L0_conv_ref(_gn(x), L0_conv_w_qkv, L0_conv_b_qkv, L0_conv_w_dw, L0_conv_b_dw, L0_conv_w_proj, L0_conv_b_proj, L0_conv_temperature)
    x = x + _L1_conv_ref(_gn(x), L1_conv_ln_w, L1_conv_ln_b, L1_conv_Wq, L1_conv_Wk, L1_conv_Wv, L1_conv_w1, L1_conv_w2)
    return x


_drawn_inputs = setup_inputs


def setup_inputs(seed=0):
    import zlib

    import numpy as np

    out = dict(_drawn_inputs(seed))
    spreads = {'L0_conv_temperature': (1.0, 0.6), 'L1_conv_ln_w': (1.0, 0.2), 'L1_conv_ln_b': (0.0, 0.1)}
    factors = {'L0_conv_w_qkv': 8.0}
    for name, (base, spread) in spreads.items():
        noise = np.random.default_rng([zlib.crc32(name.encode()), seed]).standard_normal(out[name].shape)
        drawn = base * np.exp(spread * noise) if base else spread * noise
        out[name] = jnp.asarray(drawn.astype(out[name].dtype))
    for name, factor in factors.items():
        out[name] = (out[name] * factor).astype(out[name].dtype)
    return out
```

```python
from contextlib import ExitStack

import concourse.bass as bass
from concourse import mybir

F32 = mybir.dt.float32
F16 = mybir.dt.float16
ALU = mybir.AluOpType
ACT = mybir.ActivationFunctionType
AX_X = mybir.AxisListType.X

B, C, HH, WW = 2, 192, 64, 64
N = HH * WW
HEADS, HD = 4, 48
CT, CP = 2, 96
P = 128
HALF = 64
KR = HALF + HD
CH = 512
NCH = N // CH
KT = N // P
NB = 1024
NBL = N // NB
ROWS = CH // WW
TAPS = 9
PW = WW + 2
SPLIT = 4096.0
SAFE = 60.0

TILES_PAIR = 3
PAIRS = B * HEADS // 2
CONV_OPS = 2 * TAPS

USE_FIRST = 8 + 8 + 8 + 8
USE_EVEN = 8 + 8 + 8 + 4
USE_ODD = 8 + 8 + 8 + 8 + 4
USE_PAIR = USE_EVEN + USE_ODD
DEN_AT = {1: 12, 2: 4, 3: 4}


def group_norm_and_store(nc, x, consts, z_dram):
    with ExitStack() as ctx:
        def sb(name, shape, dt=F32):
            return ctx.enter_context(nc.sbuf_tensor(name, shape, dt))

        def sem(name):
            return ctx.enter_context(nc.semaphore(name))

        NT = B * CT
        xin = sb("gn_x", [CP, NT, N])
        group = sb("gn_group", [CP, CP])
        stats = sb("gn_stats", [CP, NT, NCH, 6])
        mv = sb("gn_mv", [CP, NT, 2])
        mean = sb("gn_mean", [CP, NT])
        dev = sb("gn_dev", [CP, NT])
        var = sb("gn_var", [CP, NT])
        half = sb("gn_half", [CP, NT])
        y = sb("gn_y", [CP, NT])
        t = sb("gn_t", [CP, NT])
        ps = ctx.enter_context(nc.psum_tensor("gn_ps", [P, 2, CH], F32))
        x_in = [sem(f"gn_x_in{i}") for i in range(NT)]
        group_in = sem("gn_group_in")
        vec = sem("gn_vec")
        asked = sem("gn_asked")
        summed = sem("gn_summed")
        pow_asked = sem("gn_pow_asked")
        powed = sem("gn_powed")
        z_made = sem("gn_z_made")
        z_out = sem("gn_z_out")

        with nc.Block() as block:
            @block.sync
            def _(sp):
                for i in range(NT):
                    sp.dma_start(xin[:, i, :], x[i // CT, (i % CT) * CP:(i % CT + 1) * CP, :]).then_inc(x_in[i], 16)
                    if i == 0:
                        sp.dma_start(group[:, :], consts["group"]).then_inc(group_in, 16)
                for i in range(NT):
                    sp.wait_ge(z_made, i + 1)
                    sp.dma_start(z_dram[i // CT, (i % CT) * CP:(i % CT + 1) * CP, :], xin[:, i, :]).then_inc(z_out, 16)
                sp.wait_ge(z_out, 16 * NT)

            @block.gpsimd
            def _(pool):
                pool.memset(half[:, :], -0.5).then_inc(powed, 1)
                pool.wait_ge(powed, 1)
                pool.wait_ge(pow_asked, 1)
                pool.tensor_tensor(y[:, :], var[:, :], half[:, :], ALU.pow).then_inc(powed, 1)

            @block.tensor
            def _(pe):
                pe.wait_ge(group_in, 16)
                for k, src in enumerate((mean, var)):
                    pe.wait_ge(asked, k + 1)
                    pe.matmul(ps[0:CP, k, 0:NT], group[:, :], src[:, :], start=True, stop=True).then_inc(summed, 1)

            @block.vector
            def _(dve):
                n = [0]

                def link(ins):
                    n[0] += 1
                    ins.then_inc(vec, 1)
                    dve.wait_ge(vec, n[0])

                for i in range(NT):
                    dve.wait_ge(x_in[i], 16)
                    for c in range(NCH):
                        ins = dve.bn_stats(stats[:, i, c, :], xin[:, i, c * CH:(c + 1) * CH])
                    link(ins)
                    link(dve.bn_aggr(mv[:, i, :], stats[:, i, :, :].rearrange("p c s -> p (c s)")))
                dve.tensor_copy(mean[:, :], mv[:, :, 0]).then_inc(asked, 1)
                dve.wait_ge(summed, 1)
                dve.wait_ge(asked, 1)
                link(dve.tensor_tensor(dev[:, :], mean[:, :], ps[0:CP, 0, 0:NT], ALU.subtract))
                link(dve.tensor_copy(mean[:, :], ps[0:CP, 0, 0:NT]))
                link(dve.tensor_tensor(dev[:, :], dev[:, :], dev[:, :], ALU.mult))
                dve.tensor_tensor(var[:, :], mv[:, :, 1], dev[:, :], ALU.add).then_inc(asked, 1)
                dve.wait_ge(summed, 2)
                dve.wait_ge(asked, 2)
                dve.tensor_scalar(var[:, :], ps[0:CP, 1, 0:NT], 1e-5, None, ALU.add).then_inc(pow_asked, 1)
                dve.wait_ge(powed, 2)
                dve.wait_ge(pow_asked, 1)
                link(dve.scalar_tensor_tensor(out=t[:, :], in0=var[:, :], scalar=-0.5, in1=y[:, :], op0=ALU.mult, op1=ALU.mult))
                link(dve.tensor_tensor(t[:, :], t[:, :], y[:, :], ALU.mult))
                link(dve.scalar_tensor_tensor(out=y[:, :], in0=t[:, :], scalar=1.5, in1=y[:, :], op0=ALU.add, op1=ALU.mult))
                for i in range(NT):
                    dve.tensor_scalar(xin[:, i, :], xin[:, i, :], mean[:, i:i + 1], y[:, i:i + 1],
                                      ALU.subtract, ALU.mult).then_inc(z_made, 1)


class Uses:

    def __init__(self, base):
        self.base, self.n = base, 0

    def next(self):
        self.n += 1
        return self.base + self.n - 1, (self.n - 1) % 2


def layer0(nc, z_dram, w_qkv, vecs, temperature, consts, ss_dram, rn_dram, o_dram):
    with ExitStack() as ctx:
        def sb(name, shape, dt=F32):
            return ctx.enter_context(nc.sbuf_tensor(name, shape, dt))

        def psum(name, shape):
            return ctx.enter_context(nc.psum_tensor(name, shape, F32))

        def sem(name):
            return ctx.enter_context(nc.semaphore(name))

        ZS = 4
        z = sb("z", [CP, ZS, CT, CH])
        w = sb("w", [CP, TILES_PAIR, CT, P])
        vec = sb("vec", [P, TILES_PAIR, TAPS + 2])
        pad = sb("pad", [KR, PW, PW])
        qk = sb("qk", [KR, N])
        vv = sb("vv", [KR, N])
        sq = sb("sq", [KR, N])
        ss = sb("ss", [KR, N])
        nrm = sb("nrm", [P, 2, KT])
        nry = sb("nry", [P, 2, KT])
        nrt = sb("nrt", [P, 2, KT])
        mhalf = sb("mhalf", [P, 2, KT])
        u = sb("u", [KR, NB])
        hi = sb("hi", [KR, 2, NB], F16)
        lo = sb("lo", [KR, 2, NB], F16)
        q_hi = sb("q_hi", [KR, 2, N], F16)
        q_lo = sb("q_lo", [KR, 2, N], F16)
        k_hl = sb("k_hl", [KR, 2, N], F16)
        vt = sb("vt", [P, 2, KT, HALF])
        prob = sb("prob", [P, 2, NB])
        acc_s = sb("acc_s", [P, CH])
        rden = sb("rden", [P, CH])
        o_s = sb("o_s", [P, 2, CH])
        ident = sb("ident", [P, P])
        ones_blk = sb("ones_blk", [P, P])
        den_sel = sb("den_sel", [P, P])
        temp = sb("temp", [P, B * HEADS])
        tabs = sb("tabs", [P, B * HEADS])
        cur = sb("cur", [P, 2, 2])

        ps_s = psum("ps_s", [P, 2, NB])
        ps_a = psum("ps_a", [P, 2, CH])
        ps_h = psum("ps_h", [P, 2, CH])

        z_in = [sem(f"z_in{i}") for i in range(ZS)]
        w_in = [sem(f"w_in{i}") for i in range(TILES_PAIR)]
        const_in = sem("const_in")
        help_full = sem("help_full")
        help_free = sem("help_free")
        conv_op = sem("conv_op")
        sq_done = sem("sq_done")
        ss_out = sem("ss_out")
        ss_in = sem("ss_in")
        norm_asked = sem("norm_asked")
        powed = sem("powed")
        norm_op = sem("norm_op")
        rn_out = sem("rn_out")
        rn_in = sem("rn_in")
        unit_op = sem("unit_op")
        lo_done = sem("lo_done")
        split_in = [sem(f"split_in{i}") for i in range(2)]
        cur_set = sem("cur_set")
        scores = sem("scores")
        exped = sem("exped")
        pv_done = sem("pv_done")
        acc_free = sem("acc_free")
        o_op = sem("o_op")
        o_out = sem("o_out")
        o_stored = sem("o_stored")
        zero_set = sem("zero_set")
        vt_set = sem("vt_set")
        vstep = sem("vstep")

        STEPS = NBL * KT
        NCONST = 4

        with nc.Block() as block:
            @block.sync
            def _(sp):
                sp.dma_start(ident[:, :], consts["ident"]).then_inc(const_in, 16)
                sp.dma_start(ones_blk[:, :], consts["ones_blk"]).then_inc(const_in, 16)
                sp.dma_start(den_sel[:, :], consts["den_sel"]).then_inc(const_in, 16)
                sp.dma_start(temp[:, :], temperature.partition_broadcast(P)).then_inc(const_in, 16)

                def load_w(slot, tile):
                    sp.dma_start(w[:, slot, :, :].rearrange("p c (h o) -> p c h o", h=2)[:, :, :, 0:HD],
                                 w_qkv[tile]).then_inc(w_in[slot], 16)
                    for h in range(2):
                        sp.dma_start(vec[h * HALF:h * HALF + HD, slot, :], vecs[tile, h]).then_inc(w_in[slot], 16)

                def load_z(chunks, tile, batch, taken):
                    for c in chunks:
                        if taken is not None:
                            sp.wait_ge(help_full, taken + c % ZS)
                        sp.dma_start(z[:, c % ZS, :, :],
                                     z_dram[batch, :, c * CH:(c + 1) * CH].rearrange("(t p) n -> p t n", p=CP)
                                     ).then_inc(z_in[c % ZS], 16)

                def store_block(g, j):
                    sp.wait_ge(o_op, NBL * g + j + 2)
                    for h in range(2):
                        sp.dma_start(o_dram[g, :, j * NB + h * CH:j * NB + (h + 1) * CH],
                                     o_s[h * HALF:h * HALF + HD, j % 2, :]).then_inc(o_out, 16)
                    sp.wait_ge(o_out, 32 * (NBL * g + j + 1))
                    sp.sem_inc(o_stored, 1)

                def sums_out(free_needed, k):
                    sp.wait_ge(help_free, free_needed)
                    for h in range(2):
                        sp.dma_start(ss_dram[h:h + 1, :], ss[h * HALF:h * HALF + 1, :]).then_inc(ss_out, 16)
                    sp.wait_ge(ss_out, 32 * k + 32)
                    sp.dma_start(nrm[:, :, :], ss_dram.rearrange("h (p t) -> p h t", p=P)).then_inc(ss_in, 16)

                def norms_out(k):
                    sp.wait_ge(norm_op, 4 * k + 4)
                    sp.dma_start(rn_dram.rearrange("h (p t) -> p h t", p=P), nry[:, :, :]).then_inc(rn_out, 16)
                    sp.wait_ge(rn_out, 16 * k + 16)
                    for h in range(2):
                        sp.dma_start(sq[h * HALF:h * HALF + HD, :],
                                     rn_dram[h:h + 1, :].partition_broadcast(HD)).then_inc(rn_in, 16)

                def split_out(slot, k, scores_needed):
                    if scores_needed is not None:
                        sp.wait_ge(scores, scores_needed)
                    for c in range(4):
                        cols = slice(c * NB, (c + 1) * NB)
                        sp.wait_ge(unit_op, 8 * k + 2 * c + 2)
                        for dst, src in ((q_hi[0:HD], hi[0:HD]), (q_hi[HALF:KR], hi[0:HD]), (k_hl[0:HD], hi[HALF:KR])):
                            sp.dma_start(dst[:, slot, cols], src[:, c % 2, :]).then_inc(split_in[c % 2], 16)
                        sp.wait_ge(lo_done, 4 * k + c + 1)
                        for dst, src in ((q_lo[0:HD], lo[0:HD]), (q_lo[HALF:KR], lo[0:HD]), (k_hl[HALF:KR], lo[HALF:KR])):
                            sp.dma_start(dst[:, slot, cols], src[:, c % 2, :]).then_inc(split_in[c % 2], 16)

                sp.sem_inc(o_stored, 2)
                sp.wait_ge(zero_set, 1)
                for t in range(TILES_PAIR):
                    load_w(t, t)
                load_z(range(4), 0, 0, None)
                load_z(range(4, 8), 0, 0, 1)
                load_z(range(4), 1, 0, 5)
                sums_out(16, 0)
                load_z(range(4, 8), 1, 0, 17)
                norms_out(0)
                sp.wait_ge(zero_set, 3)
                split_out(0, 0, None)

                def pair(i, last):
                    base, g = USE_FIRST + i * USE_PAIR, 2 * i
                    if not last:
                        sp.wait_ge(conv_op, CONV_OPS * (3 * i + 2))
                        for t in range(2):
                            load_w(t, 3 * i + 3 + t)
                    load_z(range(4), 3 * i + 2, i // 2, base - 11)
                    load_z(range(4, 8), 3 * i + 2, i // 2, base + 1)
                    store_block(g, 0)
                    sums_out(base + 17, g + 1)
                    store_block(g, 1)
                    norms_out(g + 1)
                    split_out(1, g + 1, STEPS * g + 1)
                    store_block(g, 2)
                    store_block(g, 3)
                    base, g = base + USE_EVEN, g + 1
                    if not last:
                        sp.wait_ge(conv_op, CONV_OPS * (3 * i + 3))
                        load_w(2, 3 * i + 5)
                        nxt = (i + 1) // 2
                        load_z(range(4), 3 * i + 3, nxt, base)
                        load_z(range(4, 8), 3 * i + 3, nxt, base + 1)
                        load_z(range(4), 3 * i + 4, nxt, base + 5)
                    store_block(g, 0)
                    if not last:
                        sums_out(base + 17, g + 1)
                        load_z(range(4, 8), 3 * i + 4, nxt, base + 18)
                    store_block(g, 1)
                    if not last:
                        norms_out(g + 1)
                        split_out(0, g + 1, STEPS * g + 1)
                    store_block(g, 2)
                    store_block(g, 3)

                with sp.Fori(0, PAIRS - 1) as i:
                    pair(i, False)
                pair(PAIRS - 1, True)

            @block.gpsimd
            def _(pool):
                pool.memset(w[:, :, :, :], 0.0)
                pool.memset(vec[:, :, :], 0.0).then_inc(zero_set, 1)
                pool.memset(pad[:, :, :], 0.0).then_inc(zero_set, 1)
                pool.memset(q_hi[:, :, :], 0.0)
                pool.memset(q_lo[:, :, :], 0.0)
                pool.memset(k_hl[:, :, :], 0.0).then_inc(zero_set, 1)
                pool.memset(mhalf[:, :, :], -0.5).then_inc(zero_set, 1)
                pool.memset(vt[:, :, :, HD:HALF], 0.0).then_inc(vt_set, 1)
                pool.wait_ge(vt_set, 1)
                pool.memset(vt[:, :, :, HD:HD + 1], 1.0).then_inc(vt_set, 1)

                def prepare(k, convs):
                    pool.wait_ge(conv_op, CONV_OPS * convs)
                    for c in range(4):
                        cols = slice(c * NB, (c + 1) * NB)
                        pool.tensor_tensor(sq[:, cols], qk[:, cols], qk[:, cols], ALU.mult).then_inc(sq_done, 1)
                    pool.wait_ge(norm_asked, k + 1)
                    pool.tensor_tensor(nry[:, :, :], nrm[:, :, :], mhalf[:, :, :], ALU.pow).then_inc(powed, 1)
                    for c in range(4):
                        pool.wait_ge(unit_op, 8 * k + 2 * c + 2)
                        pool.tensor_tensor(lo[:, c % 2, :], u[:, :], hi[:, c % 2, :], ALU.subtract).then_inc(lo_done, 1)

                pool.wait_ge(zero_set, 4)
                prepare(0, 1)

                def pair(i, last):
                    prepare(2 * i + 1, 3 * i + 3)
                    if not last:
                        prepare(2 * i + 2, 3 * i + 4)

                with pool.Fori(0, PAIRS - 1) as i:
                    pair(i, False)
                pair(PAIRS - 1, True)

            @block.scalar
            def _(act):
                def head(slot, g):
                    act.wait_ge(cur_set, g + 1)
                    for a in range(STEPS):
                        act.wait_ge(scores, STEPS * g + a + 1)
                        if a >= 2 or not isinstance(g, int) or g > 0:
                            act.wait_ge(pv_done, STEPS * g + a - 1)
                        act.activation(prob[:, a % 2, :], ps_s[:, a % 2, :], ACT.Exp,
                                       bias=cur[:, slot, 1:2], scale=cur[:, slot, 0:1]).then_inc(exped, 1)

                act.sem_inc(exped, 2)
                head(0, 0)
                with act.Fori(0, PAIRS - 1) as i:
                    head(1, 2 * i + 1)
                    head(0, 2 * i + 2)
                head(1, 2 * PAIRS - 1)

            @block.tensor
            def _(pe):
                def project(slot, tile, c, use):
                    n, bank = use
                    helper_free(n)
                    pe.wait_ge(z_in[c % ZS], 16 * (2 * tile + c // ZS + 1))
                    for t in range(CT):
                        ins = pe.matmul(ps_h[0:KR, bank, :], w[:, slot, t, 0:KR], z[:, c % ZS, t, :],
                                        start=(t == 0), stop=(t == CT - 1))
                    ins.then_inc(help_full, 1)

                def helper_free(n):
                    if not isinstance(n, int) or n >= 2:
                        pe.wait_ge(help_free, n - 1)

                def sums(c, k, use):
                    n, bank = use
                    helper_free(n)
                    pe.wait_ge(sq_done, 4 * k + c // 2 + 1)
                    pe.matmul(ps_h[0:KR, bank, :], ones_blk[0:KR, 0:KR], sq[:, c * CH:(c + 1) * CH],
                              start=True, stop=True).then_inc(help_full, 1)

                def transpose_v(q, use):
                    n, bank = use
                    helper_free(n)
                    for m4 in range(4):
                        m = q * 4 + m4
                        ins = pe.transpose(ps_h[:, bank, m4 * P:m4 * P + KR], vv[:, m * P:(m + 1) * P], ident[0:KR, 0:KR])
                    ins.then_inc(help_full, 1)

                def denominators(g, j, use):
                    n, bank = use
                    helper_free(n)
                    pe.wait_ge(acc_free, NBL * g + j + 3)
                    pe.matmul(ps_h[:, bank, :], den_sel[:, :], acc_s[:, :], start=True, stop=True).then_inc(help_full, 1)

                uses = Uses(0)
                pe.wait_ge(const_in, 16 * NCONST)
                pe.wait_ge(w_in[0], 48)
                for c in range(8):
                    project(0, 0, c, uses.next())
                for c in range(8):
                    sums(c, 0, uses.next())
                pe.wait_ge(w_in[1], 48)
                for c in range(8):
                    project(1, 1, c, uses.next())
                pe.wait_ge(conv_op, CONV_OPS * 2)
                for q in range(8):
                    transpose_v(q, uses.next())

                def head(slot, g, base, late, prep):
                    uses = Uses(base)
                    pe.wait_ge(help_free, base - late)
                    for c in range(2):
                        pe.wait_ge(split_in[c], 96 * 2 * (g + 1))

                    def score(a):
                        j, m = a // KT, a % KT
                        pe.wait_ge(exped, STEPS * g + a + 1)
                        for h in range(2):
                            cols = slice(j * NB + h * CH, j * NB + (h + 1) * CH)
                            for t, q in enumerate((q_hi, q_lo)):
                                ins = pe.matmul(ps_s[:, a % 2, h * CH:(h + 1) * CH], k_hl[:, slot, m * P:(m + 1) * P],
                                                q[:, slot, cols], start=(t == 0), stop=(t == 1))
                        ins.then_inc(scores, 1)

                    def weigh(a):
                        j, m = a // KT, a % KT
                        pe.wait_ge(exped, STEPS * g + a + 3)
                        if m == 0:
                            pe.wait_ge(acc_free, NBL * g + j + 1)
                        for h in range(2):
                            ins = pe.matmul(ps_a[h * HALF:(h + 1) * HALF, j % 2, :], vt[:, slot, m, :],
                                            prob[:, a % 2, h * CH:(h + 1) * CH], start=(m == 0), stop=(m == KT - 1))
                        ins.then_inc(pv_done, 1)

                    score(0)
                    for a in range(STEPS):
                        j, m = a // KT, a % KT
                        if a + 1 < STEPS:
                            score(a + 1)
                        weigh(a)
                        prep(j, m, uses)
                        if j >= 1 and m == DEN_AT[j]:
                            denominators(g, j - 1, uses.next())
                    denominators(g, NBL - 1, uses.next())

                def even(i):
                    def prep(j, m, uses):
                        if j == 0 and m in range(3, 19, 2):
                            if m == 3:
                                pe.wait_ge(w_in[2], 48 * (i + 1))
                            project(2, 3 * i + 2, (m - 3) // 2, uses.next())
                        if j == 1 and m in range(14, 30, 2):
                            sums((m - 14) // 2, 2 * i + 1, uses.next())
                        if j == 3 and m in range(8, 24, 2):
                            transpose_v((m - 8) // 2, uses.next())
                    head(0, 2 * i, USE_FIRST + i * USE_PAIR, 0, prep)

                def odd(i, last):
                    def prep(j, m, uses):
                        if last:
                            return
                        if j == 0 and m in range(3, 19, 2):
                            if m == 3:
                                pe.wait_ge(w_in[0], 48 * (i + 2))
                            project(0, 3 * i + 3, (m - 3) // 2, uses.next())
                        if j == 1 and m in range(14, 22):
                            sums(m - 14, 2 * i + 2, uses.next())
                        if j == 1 and m in range(22, 30):
                            if m == 22:
                                pe.wait_ge(w_in[1], 48 * (i + 2))
                            project(1, 3 * i + 4, m - 22, uses.next())
                        if j == 3 and m in range(16, 32, 2):
                            if m == 16:
                                pe.wait_ge(conv_op, CONV_OPS * (3 * i + 5))
                            transpose_v((m - 16) // 2, uses.next())
                    head(1, 2 * i + 1, USE_FIRST + i * USE_PAIR + USE_EVEN, 1, prep)

                with pe.Fori(0, PAIRS - 1) as i:
                    even(i)
                    odd(i, False)
                even(PAIRS - 1)
                odd(PAIRS - 1, True)

            @block.vector
            def _(dve):
                def full(n):
                    dve.wait_ge(help_full, n + 1)

                def evac_project(slot, c, use):
                    n, bank = use
                    full(n)
                    rows = slice(1 + c * ROWS, 1 + (c + 1) * ROWS)
                    dve.tensor_scalar(pad[:, rows, 1:WW + 1], ps_h[0:KR, bank, :].rearrange("p (r c) -> p r c", c=WW),
                                      vec[0:KR, slot, 0:1], None, ALU.add).then_inc(help_free, 1)

                def conv(slot, dst, tiles, n_free):
                    dve.wait_ge(help_free, n_free)
                    for tap in range(TAPS):
                        dy, dx = tap // 3, tap % 3
                        for h in range(2):
                            r0 = h * (HH // 2)
                            src = pad[:, r0 + dy:r0 + dy + HH // 2, dx:dx + WW]
                            out = dst[:, h * N // 2:(h + 1) * N // 2].rearrange("p (r c) -> p r c", c=WW)
                            if tap == 0:
                                ins = dve.tensor_scalar(out, src, vec[0:KR, slot, 1:2], vec[0:KR, slot, 10:11],
                                                        ALU.mult, ALU.add)
                            else:
                                dve.wait_ge(conv_op, CONV_OPS * tiles + 2 * tap + h - 1)
                                ins = dve.scalar_tensor_tensor(out=out, in0=src, scalar=vec[0:KR, slot, 1 + tap:2 + tap],
                                                               in1=out, op0=ALU.mult, op1=ALU.add)
                            ins.then_inc(conv_op, 1)

                def evac_sums(c, use):
                    n, bank = use
                    full(n)
                    dve.tensor_copy(ss[:, c * CH:(c + 1) * CH], ps_h[0:KR, bank, :]).then_inc(help_free, 1)

                def norms(k):
                    dve.wait_ge(ss_in, 16 * k + 16)
                    if not (isinstance(k, int) and k == 0):
                        dve.wait_ge(rn_out, 16 * k)
                    dve.tensor_scalar(nrm[:, :, :], nrm[:, :, :], 1e-24, None, ALU.max).then_inc(norm_asked, 1)
                    dve.wait_ge(norm_asked, k + 1)
                    dve.wait_ge(powed, k + 1)
                    dve.scalar_tensor_tensor(out=nrt[:, :, :], in0=nrm[:, :, :], scalar=-0.5, in1=nry[:, :, :],
                                             op0=ALU.mult, op1=ALU.mult).then_inc(norm_op, 1)
                    dve.wait_ge(norm_op, 4 * k + 1)
                    dve.tensor_tensor(nrt[:, :, :], nrt[:, :, :], nry[:, :, :], ALU.mult).then_inc(norm_op, 1)
                    dve.wait_ge(norm_op, 4 * k + 2)
                    dve.scalar_tensor_tensor(out=nry[:, :, :], in0=nrt[:, :, :], scalar=1.5, in1=nry[:, :, :],
                                             op0=ALU.add, op1=ALU.mult).then_inc(norm_op, 1)
                    dve.wait_ge(norm_op, 4 * k + 3)
                    dve.tensor_scalar(nry[:, :, :], nry[:, :, :], SPLIT, None, ALU.mult).then_inc(norm_op, 1)

                def split(k):
                    dve.wait_ge(rn_in, 32 * k + 32)
                    for c in range(4):
                        cols = slice(c * NB, (c + 1) * NB)
                        if c >= 1:
                            dve.wait_ge(lo_done, 4 * k + c)
                        elif not (isinstance(k, int) and k == 0):
                            dve.wait_ge(lo_done, 4 * k)
                        for h in range(2):
                            r = slice(h * HALF, h * HALF + HD)
                            ins = dve.tensor_tensor(u[r, :], qk[r, cols], sq[r, cols], ALU.mult)
                        ins.then_inc(unit_op, 1)
                        dve.wait_ge(unit_op, 8 * k + 2 * c + 1)
                        if c >= 2 or not (isinstance(k, int) and k == 0):
                            dve.wait_ge(split_in[c % 2], 96 * (2 * k + c // 2))
                        dve.tensor_copy(hi[:, c % 2, :], u[:, :]).then_inc(unit_op, 1)

                def evac_vt(slot, q, use):
                    n, bank = use
                    full(n)
                    dve.tensor_copy(vt[:, slot, q * 4:(q + 1) * 4, 0:HD],
                                    ps_h[:, bank, :].rearrange("p (m d) -> p m d", d=P)[:, :, slot * HALF:slot * HALF + HD]
                                    ).then_inc(help_free, 1)

                def set_cur(slot, g):
                    dve.wait_ge(vstep, 4)
                    if not (isinstance(g, int) and g == 0):
                        dve.wait_ge(exped, STEPS * (g - 1) + 3)
                    dve.tensor_copy(cur[:, slot, 0:1], temp[:, bass.ds(g, 1)])
                    dve.tensor_copy(cur[:, slot, 1:2], tabs[:, bass.ds(g, 1)]).then_inc(cur_set, 1)

                def copy_acc(g, j):
                    dve.wait_ge(pv_done, STEPS * g + KT * (j + 1))
                    dve.wait_ge(o_op, NBL * g + j + 1)
                    dve.tensor_copy(acc_s[:, :], ps_a[:, j % 2, :]).then_inc(acc_free, 1)

                def finish(g, j, use):
                    n, bank = use
                    full(n)
                    dve.reciprocal(rden[:, :], ps_h[:, bank, :]).then_inc(help_free, 1)
                    dve.wait_ge(help_free, n + 1)
                    dve.wait_ge(o_stored, NBL * g + j + 1)
                    dve.tensor_tensor(o_s[:, j % 2, :], acc_s[:, :], rden[:, :], ALU.mult).then_inc(o_op, 1)

                dve.sem_inc(acc_free, 2)
                dve.sem_inc(o_op, 1)
                dve.wait_ge(const_in, 16 * NCONST)
                dve.tensor_scalar(tabs[:, :], temp[:, :], -1.0, None, ALU.mult).then_inc(vstep, 1)
                dve.wait_ge(vstep, 1)
                dve.tensor_tensor(tabs[:, :], tabs[:, :], temp[:, :], ALU.max).then_inc(vstep, 1)
                dve.wait_ge(vstep, 2)
                dve.tensor_scalar(tabs[:, :], tabs[:, :], -1.0, SAFE, ALU.mult, ALU.add).then_inc(vstep, 1)
                dve.wait_ge(vstep, 3)
                dve.tensor_scalar(tabs[:, :], tabs[:, :], 0.0, None, ALU.min)
                dve.tensor_scalar(temp[:, :], temp[:, :], 1.0 / (SPLIT * SPLIT), None, ALU.mult).then_inc(vstep, 1)
                set_cur(0, 0)

                dve.memset(u[:, :], 0.0).then_inc(vstep, 1)
                dve.wait_ge(vstep, 5)

                dve.wait_ge(zero_set, 2)
                uses = Uses(0)
                dve.wait_ge(w_in[0], 48)
                for c in range(8):
                    evac_project(0, c, uses.next())
                conv(0, qk, 0, 8)
                for c in range(8):
                    evac_sums(c, uses.next())
                dve.wait_ge(w_in[1], 48)
                for c in range(8):
                    evac_project(1, c, uses.next())
                norms(0)
                conv(1, vv, 1, 24)
                split(0)
                dve.wait_ge(vt_set, 2)
                for q in range(8):
                    evac_vt(0, q, uses.next())

                def even(i):
                    uses = Uses(USE_FIRST + i * USE_PAIR)
                    g = 2 * i
                    set_cur(1, g + 1)
                    dve.wait_ge(w_in[2], 48 * (i + 1))
                    for c in range(8):
                        evac_project(2, c, uses.next())
                    conv(2, qk, 3 * i + 2, uses.base + uses.n)
                    copy_acc(g, 0)
                    finish(g, 0, uses.next())
                    for c in range(8):
                        evac_sums(c, uses.next())
                    copy_acc(g, 1)
                    finish(g, 1, uses.next())
                    norms(g + 1)
                    split(g + 1)
                    copy_acc(g, 2)
                    finish(g, 2, uses.next())
                    dve.wait_ge(pv_done, STEPS * g + 1)
                    for q in range(8):
                        evac_vt(1, q, uses.next())
                    copy_acc(g, 3)
                    finish(g, 3, uses.next())

                def odd(i, last):
                    uses = Uses(USE_FIRST + i * USE_PAIR + USE_EVEN)
                    g = 2 * i + 1
                    if not last:
                        set_cur(0, g + 1)
                        dve.wait_ge(w_in[0], 48 * (i + 2))
                        for c in range(8):
                            evac_project(0, c, uses.next())
                        conv(0, qk, 3 * i + 3, uses.base + uses.n)
                    copy_acc(g, 0)
                    finish(g, 0, uses.next())
                    if not last:
                        for c in range(8):
                            evac_sums(c, uses.next())
                        dve.wait_ge(w_in[1], 48 * (i + 2))
                        for c in range(8):
                            evac_project(1, c, uses.next())
                        v_uses = uses.base + uses.n
                    copy_acc(g, 1)
                    finish(g, 1, uses.next())
                    if not last:
                        norms(g + 1)
                        conv(1, vv, 3 * i + 4, v_uses)
                        split(g + 1)
                    copy_acc(g, 2)
                    finish(g, 2, uses.next())
                    if not last:
                        dve.wait_ge(pv_done, STEPS * g + 1)
                        for q in range(8):
                            evac_vt(0, q, uses.next())
                    copy_acc(g, 3)
                    finish(g, 3, uses.next())

                with dve.Fori(0, PAIRS - 1) as i:
                    even(i)
                    odd(i, False)
                even(PAIRS - 1)
                odd(PAIRS - 1, True)


def layer1(nc, x, o_dram, weights, consts, m_dram, r_dram, out):
    with ExitStack() as ctx:
        def sb(name, shape, dt=F32):
            return ctx.enter_context(nc.sbuf_tensor(name, shape, dt))

        def psum(name, shape):
            return ctx.enter_context(nc.psum_tensor(name, shape, F32))

        def sem(name):
            return ctx.enter_context(nc.semaphore(name))

        QB = 1024
        NQ = N // QB
        RB = KT
        GR = 4
        NG = KT // GR
        PRO = 8 * 5 + 8
        USE = PRO + RB * NQ

        xg = sb("xg", [CP, CT, N])
        gp = sb("gp", [P, CT, N])
        g = gp[0:CP, :, :]
        prob = [gp[:, s, :] for s in range(2)]
        vb = sb("vb", [P, N])
        rn = sb("rn", [P, N])
        q = sb("q", [CP, CT, N])
        k = sb("k", [CP, CT, N])
        v = sb("v", [P, KT, C])
        qs = sb("qs", [CP, 2, CT, P])
        at = sb("at", [P, 4, GR * P])
        wq = sb("wq", [CP, CT, C])
        wk = sb("wk", [CP, CT, C])
        wv = sb("wv", [CP, CT, C])
        wp = sb("wp", [CP, CT, C])
        pvec = sb("pvec", [CP, CT, 3])
        mixw = sb("mixw", [P, 2])
        mix = sb("mix", [P, 8])
        mtmp = sb("mtmp", [P, 2])
        group = sb("group1", [CP, CP])
        meanm = sb("meanm", [CP, CP])
        ident = sb("ident1", [P, P])
        stats = sb("stats", [CP, CT, NCH, 6])
        mv = sb("mv", [CP, CT, 2])
        gst = sb("gst", [CP, 5, CT])
        mhalf = sb("mhalf1", [P, KT])
        tv = sb("tv", [P, KT])
        ty = sb("ty", [P, KT])
        tt = sb("tt", [P, KT])
        mx = sb("mx", [P, 2, NQ])
        nbias = sb("nbias", [P, 2])
        sums = sb("sums", [P, 2, NQ])
        coef = sb("coef", [P, 2])
        ob = sb("ob", [P, C])
        ot = sb("ot", [CP, 2, CT, P])

        o_in_buf = q
        x_in_buf = k
        sq_buf = q

        ps_s = psum("ps_s1", [P, 2, QB])
        ps_t = psum("ps_t1", [P, 2, CH])
        ps_o = psum("ps_o1", [P, CH])
        ps_f = psum("ps_f1", [P, CH])

        const_in = sem("const_in1")
        chunk_in = [sem(f"chunk_in{i}") for i in range(4)]
        s_full = sem("s_full")
        s_free = sem("s_free")
        stat = sem("stat")
        f_full = sem("f_full")
        pow_asked = sem("pow_asked1")
        powed = sem("powed1")
        g_ready = sem("g_ready")
        g_made = sem("g_made")
        xg_made = sem("xg_made")
        dev_made = sem("dev_made")
        sq_made = sem("sq_made1")
        v_out = sem("v_out")
        v_in = sem("v_in")
        tok = sem("tok")
        r_out = sem("r_out")
        r_in = sem("r_in")
        ln_op = sem("ln_op")
        mix_op = sem("mix_op")
        mix_exp = sem("mix_exp")
        qs_set = sem("qs_set")
        mx_op = sem("mx_op")
        exped = sem("exped1")
        r_op = sem("r_op")
        c_op = sem("c_op")
        p_made = sem("p_made")
        t_full = sem("t_full")
        t_free = sem("t_free")
        w_done = sem("w_done")
        ob_made = sem("ob_made")
        ot_made = sem("ot_made")
        ot_out = sem("ot_out")
        ot_stored = sem("ot_stored")

        NCONST = 9
        SQ0 = 4 * CH
        STAT, TOK, LN = 8, 4, 4 * NCH

        with nc.Block() as block:
            @block.sync
            def _(sp):
                for dst, src in ((wp, weights["wp"]), (wq, weights["wq"]), (wk, weights["wk"]), (wv, weights["wv"])):
                    sp.dma_start(dst[:, :, :], src).then_inc(const_in, 16)
                sp.dma_start(pvec[:, :, :], weights["pvec"]).then_inc(const_in, 16)
                sp.dma_start(mixw[:, :], weights["mix"].partition_broadcast(P)).then_inc(const_in, 16)
                sp.dma_start(group[:, :], consts["group"]).then_inc(const_in, 16)
                sp.dma_start(meanm[:, :], consts["mean"]).then_inc(const_in, 16)
                sp.dma_start(ident[:, :], consts["ident"]).then_inc(const_in, 16)
                sp.sem_inc(ot_stored, 2)

                def image(b, later):
                    if later:
                        sp.wait_ge(s_full, b * USE)
                    for c in range(NCH):
                        s = c % 4
                        if c >= 4:
                            sp.wait_ge(stat, (STAT + NCH) * b + c - 3)
                        cols = slice(c * CH, (c + 1) * CH)
                        for buf, src in ((o_in_buf, o_dram[b]), (x_in_buf, x[b])):
                            sp.dma_start(buf[:, :, s * CH:(s + 1) * CH],
                                         src[:, cols].rearrange("(t p) n -> p t n", p=CP)).then_inc(chunk_in[s], 16)
                    sp.wait_ge(s_free, b * USE + 2 + 24)
                    sp.dma_start(m_dram, vb[0:1, :]).then_inc(v_out, 16)
                    sp.wait_ge(v_out, 16 * b + 16)
                    sp.dma_start(tv[:, :], m_dram.rearrange("o (p t) -> (o p) t", p=P)).then_inc(v_in, 16)
                    sp.wait_ge(tok, TOK * b + 4)
                    sp.dma_start(r_dram.rearrange("o (p t) -> (o p) t", p=P), ty[:, :]).then_inc(r_out, 16)
                    sp.wait_ge(r_out, 16 * b + 16)
                    sp.dma_start(rn[0:CP, :], r_dram.partition_broadcast(CP)).then_inc(r_in, 16)

                    def store(r):
                        for s in range(2):
                            row = RB * b + 2 * r + s
                            sp.wait_ge(ot_made, row + 1)
                            sp.dma_start(out[b, :, bass.ds((2 * r + s) * P, P)].rearrange("(t p) n -> p t n", p=CP),
                                         ot[:, s, :, :]).then_inc(ot_out, 16)
                            sp.wait_ge(ot_out, 16 * row + 16)
                            sp.sem_inc(ot_stored, 1)

                    with sp.Fori(0, RB // 2) as r:
                        store(r)

                for b in range(B):
                    image(b, b > 0)

            @block.gpsimd
            def _(pool):
                pool.memset(mhalf[:, :], -0.5).then_inc(powed, 1)
                pool.wait_ge(powed, 1)
                pool.wait_ge(pow_asked, 1)
                pool.tensor_tensor(mix[:, 6:7], mix[:, 5:6], mhalf[:, 0:1], ALU.pow).then_inc(powed, 1)

                for b in range(B):
                    pool.wait_ge(pow_asked, 2 * b + 2)
                    pool.tensor_tensor(gst[:, 3, :], gst[:, 2, :], mhalf[0:CP, 0:CT], ALU.pow).then_inc(powed, 1)
                    pool.wait_ge(g_made, CT * b + CT)
                    for c in range(NCH):
                        cols = slice(c * CH, (c + 1) * CH)
                        pool.tensor_tensor(xg[:, :, cols], xg[:, :, cols], g[:, :, cols], ALU.add).then_inc(xg_made, 1)
                    pool.wait_ge(pow_asked, 2 * b + 3)
                    pool.tensor_tensor(ty[:, :], tv[:, :], mhalf[:, :], ALU.pow).then_inc(powed, 1)

                    pool.wait_ge(s_free, b * USE + 2 + PRO)
                    with pool.Fori(0, RB // 2) as r:
                        for s in range(2):
                            row = 2 * r + s
                            pool.wait_ge(s_full, b * USE + PRO + NQ * (row - 1))
                            pool.tensor_copy(qs[:, s, :, :], q[:, :, bass.ds(row * P, P)]).then_inc(qs_set, 1)

            @block.scalar
            def _(act):
                act.wait_ge(const_in, 16 * NCONST)
                act.activation(mix[:, 0:2], mixw[:, :], ACT.Exp).then_inc(mix_exp, 1)
                act.sem_inc(t_free, 2)

                def copy_group(b, row, j):
                    act.wait_ge(t_full, NG * (RB * b + row) + j + 1)
                    act.wait_ge(w_done, NG * (RB * b + row) + j + 1)
                    act.activation(at[:, j % 4, :], ps_t[:, j % 2, :], ACT.Copy).then_inc(t_free, 1)

                def exp_piece(b, row, s, c):
                    if c == 0:
                        act.wait_ge(mx_op, 2 * (RB * b + row) + 2)
                    act.activation(prob[s][:, c * QB:(c + 1) * QB],
                                   vb[:, c * QB:(c + 1) * QB], ACT.Exp, bias=nbias[:, s:s + 1], scale=mix[:, 6:7],
                                   accum_out=sums[:, s, c:c + 1]).then_inc(exped, 1)

                for b in range(B):
                    for c in range(NCH):
                        act.wait_ge(dev_made, NCH * b + c + 1)
                        if c >= 2:
                            act.wait_ge(s_full, b * USE + 16 + c - 1)
                        act.activation(sq_buf[:, :, SQ0 + (c % 2) * CH:SQ0 + (c % 2 + 1) * CH],
                                       g[:, :, c * CH:(c + 1) * CH], ACT.Square).then_inc(sq_made, 1)
                    for c in range(NQ):
                        exp_piece(b, 0, 0, c)

                    def rows(row, s, last):
                        for j in range(NG):
                            copy_group(b, row, j)
                            if j % 2 and not last:
                                exp_piece(b, row + 1, 1 - s, j // 2)

                    with act.Fori(0, RB // 2 - 1) as r:
                        rows(2 * r, 0, False)
                        rows(2 * r + 1, 1, False)
                    rows(RB - 2, 0, False)
                    rows(RB - 1, 1, True)

            @block.tensor
            def _(pe):
                pe.wait_ge(const_in, 16 * NCONST)
                pe.sem_inc(w_done, 4)

                for b in range(B):
                    n = [0]

                    def pair_free():
                        n[0] += 1
                        pe.wait_ge(s_free, b * USE + n[0])
                        return (n[0] - 1) % 2

                    for c in range(NCH):
                        s = c % 4
                        pe.wait_ge(chunk_in[s], 32 * (2 * b + c // 4 + 1))
                        i = pair_free()
                        for o in range(CT):
                            for t in range(CT):
                                ins = pe.matmul(ps_s[0:CP, i, o * CH:(o + 1) * CH], wp[:, t, o * CP:(o + 1) * CP],
                                                o_in_buf[:, t, s * CH:(s + 1) * CH], start=(t == 0), stop=(t == CT - 1))
                        ins.then_inc(s_full, 1)
                    for j, src in enumerate((0, 2)):
                        pe.wait_ge(stat, (STAT + NCH) * b + NCH + (2 if j == 0 else 6))
                        pe.matmul(ps_f[0:CP, j * 8:j * 8 + CT], group[:, :], gst[:, src, :], start=True, stop=True).then_inc(f_full, 1)
                    pe.wait_ge(g_made, CT * b + CT)
                    for c in range(NCH):
                        i = pair_free()
                        for t in range(CT):
                            ins = pe.matmul(ps_s[0:CP, i, 0:CH], meanm[:, :], g[:, t, c * CH:(c + 1) * CH],
                                            start=(t == 0), stop=(t == CT - 1))
                        ins.then_inc(s_full, 1)
                    for c in range(NCH):
                        pe.wait_ge(sq_made, NCH * b + c + 1)
                        i = pair_free()
                        for t in range(CT):
                            ins = pe.matmul(ps_s[0:CP, i, 0:CH], meanm[:, :],
                                            sq_buf[:, t, SQ0 + (c % 2) * CH:SQ0 + (c % 2 + 1) * CH],
                                            start=(t == 0), stop=(t == CT - 1))
                        ins.then_inc(s_full, 1)
                    for c in range(NCH):
                        pe.wait_ge(ln_op, LN * b + 4 * c + 4)
                        for wm in (wk, wq):
                            i = pair_free()
                            for o in range(CT):
                                for t in range(CT):
                                    ins = pe.matmul(ps_s[0:CP, i, o * CH:(o + 1) * CH], wm[:, t, o * CP:(o + 1) * CP],
                                                    g[:, t, c * CH:(c + 1) * CH], start=(t == 0), stop=(t == CT - 1))
                            ins.then_inc(s_full, 1)
                        i = pair_free()
                        for m in range(4):
                            for t in range(CT):
                                ins = pe.matmul(ps_s[:, i, m * 256:m * 256 + C], g[:, t, (4 * c + m) * P:(4 * c + m + 1) * P],
                                                wv[:, t, :], start=(t == 0), stop=(t == CT - 1))
                        ins.then_inc(s_full, 1)

                    def scores(row, s):
                        pe.wait_ge(qs_set, RB * b + row + 1)
                        for c in range(NQ):
                            pe.wait_ge(s_free, b * USE + PRO + NQ * row + c + 1)
                            for h in range(2):
                                cols = slice(c * QB + h * CH, c * QB + (h + 1) * CH)
                                for t in range(CT):
                                    ins = pe.matmul(ps_s[:, c % 2, h * CH:(h + 1) * CH], qs[:, s, t, :], k[:, t, cols],
                                                    start=(t == 0), stop=(t == CT - 1))
                            ins.then_inc(s_full, 1)

                    def transpose_group(row, s, j):
                        pe.wait_ge(t_free, NG * (RB * b + row) + j + 1)
                        for m in range(GR):
                            cols = slice((j * GR + m) * P, (j * GR + m + 1) * P)
                            ins = pe.transpose(ps_t[:, j % 2, m * P:(m + 1) * P], prob[s][:, cols], ident[:, :])
                        ins.then_inc(t_full, 1)

                    def weigh_group(row, j):
                        pe.wait_ge(t_free, NG * (RB * b + row) + j + 3)
                        if j == 0:
                            pe.wait_ge(ob_made, RB * b + row + 1)
                        for m in range(GR):
                            kt = j * GR + m
                            ins = pe.matmul(ps_o[:, 0:C], at[:, j % 4, m * P:(m + 1) * P], v[:, kt, :],
                                            start=(kt == 0), stop=(kt == KT - 1))
                        ins.then_inc(w_done, 1)

                    def weigh(row, s):
                        pe.wait_ge(p_made, RB * b + row + 1)
                        transpose_group(row, s, 0)
                        transpose_group(row, s, 1)
                        for j in range(NG):
                            weigh_group(row, j)
                            if j + 2 < NG:
                                transpose_group(row, s, j + 2)

                    def turn_output(row):
                        pe.wait_ge(ob_made, RB * b + row + 2)
                        for t in range(CT):
                            ins = pe.transpose(ps_f[0:CP, t * P:(t + 1) * P], ob[:, t * CP:(t + 1) * CP], ident[:, :])
                        ins.then_inc(f_full, 1)

                    scores(0, 0)
                    scores(1, 1)
                    weigh(0, 0)
                    with pe.Fori(0, RB // 2 - 1) as r:
                        scores(2 * r + 2, 0)
                        turn_output(2 * r)
                        weigh(2 * r + 1, 1)
                        scores(2 * r + 3, 1)
                        turn_output(2 * r + 1)
                        weigh(2 * r + 2, 0)
                    turn_output(RB - 2)
                    weigh(RB - 1, 1)
                    turn_output(RB - 1)

            @block.vector
            def _(dve):
                dve.sem_inc(s_free, 2)
                dve.sem_inc(ob_made, 1)
                dve.wait_ge(const_in, 16 * NCONST)
                m = [0]

                def mix_step(ins):
                    m[0] += 1
                    ins.then_inc(mix_op, 1)
                    dve.wait_ge(mix_op, m[0])

                dve.wait_ge(mix_exp, 1)
                mix_step(dve.tensor_tensor(mix[:, 2:3], mix[:, 0:1], mix[:, 1:2], ALU.add))
                mix_step(dve.reciprocal(mix[:, 3:4], mix[:, 2:3]))
                mix_step(dve.tensor_scalar(mix[:, 4:6], mix[:, 0:2], mix[:, 3:4], None, ALU.mult))
                dve.tensor_scalar(mix[:, 5:6], mix[:, 5:6], 1e-30, None, ALU.max).then_inc(pow_asked, 1)
                dve.wait_ge(pow_asked, 1)
                dve.wait_ge(powed, 2)
                mix_step(dve.scalar_tensor_tensor(out=mtmp[:, 0:1], in0=mix[:, 5:6], scalar=-0.5, in1=mix[:, 6:7], op0=ALU.mult, op1=ALU.mult))
                mix_step(dve.tensor_tensor(mtmp[:, 1:2], mtmp[:, 0:1], mix[:, 6:7], ALU.mult))
                mix_step(dve.scalar_tensor_tensor(out=mix[:, 6:7], in0=mtmp[:, 1:2], scalar=1.5, in1=mix[:, 6:7], op0=ALU.add, op1=ALU.mult))
                mix_step(dve.tensor_tensor(mix[:, 7:8], mix[:, 5:6], mix[:, 6:7], ALU.mult))

                for b in range(B):
                    n = [0]
                    st = [(STAT + NCH) * b]

                    def full():
                        n[0] += 1
                        dve.wait_ge(s_full, b * USE + n[0])
                        return (n[0] - 1) % 2

                    def stat_step(ins):
                        st[0] += 1
                        ins.then_inc(stat, 1)
                        dve.wait_ge(stat, st[0])

                    for c in range(NCH):
                        s = c % 4
                        cols = slice(c * CH, (c + 1) * CH)
                        i = full()
                        for t in range(CT):
                            ins = dve.scalar_tensor_tensor(out=xg[:, t, cols], in0=ps_s[0:CP, i, t * CH:(t + 1) * CH],
                                                           scalar=pvec[:, t, 0:1], in1=x_in_buf[:, t, s * CH:(s + 1) * CH],
                                                           op0=ALU.add, op1=ALU.add)
                        ins.then_inc(s_free, 1)
                        dve.wait_ge(s_free, b * USE + 2 + n[0])
                        for t in range(CT):
                            ins = dve.bn_stats(stats[:, t, c, :], xg[:, t, cols])
                        stat_step(ins)
                    for t in range(CT):
                        ins = dve.bn_aggr(mv[:, t, :], stats[:, t, :, :].rearrange("p c s -> p (c s)"))
                    stat_step(ins)
                    stat_step(dve.tensor_copy(gst[:, 0, :], mv[:, :, 0]))
                    fb = (2 + RB) * b
                    dve.wait_ge(f_full, fb + 1)
                    stat_step(dve.tensor_tensor(gst[:, 1, :], gst[:, 0, :], ps_f[0:CP, 0:CT], ALU.subtract))
                    stat_step(dve.tensor_copy(gst[:, 0, :], ps_f[0:CP, 0:CT]))
                    stat_step(dve.tensor_tensor(gst[:, 1, :], gst[:, 1, :], gst[:, 1, :], ALU.mult))
                    stat_step(dve.tensor_tensor(gst[:, 2, :], gst[:, 1, :], mv[:, :, 1], ALU.add))
                    dve.wait_ge(f_full, fb + 2)
                    dve.tensor_scalar(gst[:, 2, :], ps_f[0:CP, 8:8 + CT], 1e-5, None, ALU.add).then_inc(pow_asked, 1)
                    dve.wait_ge(pow_asked, 2 * b + 2)
                    dve.wait_ge(powed, 2 * b + 3)
                    dve.scalar_tensor_tensor(out=gst[:, 4, :], in0=gst[:, 2, :], scalar=-0.5, in1=gst[:, 3, :],
                                             op0=ALU.mult, op1=ALU.mult).then_inc(stat, 1)
                    st[0] += 1
                    dve.wait_ge(stat, st[0])
                    dve.tensor_tensor(gst[:, 4, :], gst[:, 4, :], gst[:, 3, :], ALU.mult).then_inc(stat, 1)
                    st[0] += 1
                    dve.wait_ge(stat, st[0])
                    dve.scalar_tensor_tensor(out=gst[:, 3, :], in0=gst[:, 4, :], scalar=1.5, in1=gst[:, 3, :],
                                             op0=ALU.add, op1=ALU.mult).then_inc(g_ready, 1)
                    dve.wait_ge(g_ready, b + 1)
                    for t in range(CT):
                        dve.tensor_scalar(g[:, t, :], xg[:, t, :], gst[:, 0, t:t + 1], gst[:, 3, t:t + 1],
                                          ALU.subtract, ALU.mult).then_inc(g_made, 1)
                    dve.wait_ge(g_made, CT * b + CT)
                    for c in range(NCH):
                        cols = slice(c * CH, (c + 1) * CH)
                        i = full()
                        dve.wait_ge(xg_made, NCH * b + c + 1)
                        for t in range(CT):
                            ins = dve.tensor_tensor(g[:, t, cols], g[:, t, cols], ps_s[0:CP, i, 0:CH], ALU.subtract)
                        ins.then_inc(dev_made, 1)
                        dve.wait_ge(dev_made, NCH * b + c + 1)
                        dve.sem_inc(s_free, 1)
                    for c in range(NCH):
                        i = full()
                        dve.tensor_copy(vb[0:CP, c * CH:(c + 1) * CH], ps_s[0:CP, i, 0:CH]).then_inc(s_free, 1)
                    dve.wait_ge(v_in, 16 * b + 16)
                    if b:
                        dve.wait_ge(r_out, 16 * b)
                    dve.tensor_scalar(tv[:, :], tv[:, :], 1e-5, None, ALU.add).then_inc(pow_asked, 1)
                    dve.wait_ge(pow_asked, 2 * b + 3)
                    dve.wait_ge(powed, 2 * b + 4)
                    dve.scalar_tensor_tensor(out=tt[:, :], in0=tv[:, :], scalar=-0.5, in1=ty[:, :],
                                             op0=ALU.mult, op1=ALU.mult).then_inc(tok, 1)
                    dve.wait_ge(tok, TOK * b + 1)
                    dve.tensor_tensor(tt[:, :], tt[:, :], ty[:, :], ALU.mult).then_inc(tok, 1)
                    dve.wait_ge(tok, TOK * b + 2)
                    dve.scalar_tensor_tensor(out=ty[:, :], in0=tt[:, :], scalar=1.5, in1=ty[:, :],
                                             op0=ALU.add, op1=ALU.mult).then_inc(tok, 2)
                    dve.wait_ge(r_in, 16 * b + 16)

                    def copies(c):
                        cols = slice(c * CH, (c + 1) * CH)
                        i = full()
                        dve.tensor_copy(k[:, :, cols], ps_s[0:CP, i, :].rearrange("p (t n) -> p t n", t=CT)).then_inc(s_free, 1)
                        i = full()
                        dve.tensor_scalar(q[:, :, cols], ps_s[0:CP, i, :].rearrange("p (t n) -> p t n", t=CT),
                                          mix[0:CP, 7:8], None, ALU.mult).then_inc(s_free, 1)
                        i = full()
                        dve.tensor_copy(v[:, 4 * c:4 * c + 4, :],
                                        ps_s[:, i, :].rearrange("p (m d) -> p m d", m=4)[:, :, 0:C]).then_inc(s_free, 1)

                    for c in range(NCH):
                        cols = slice(c * CH, (c + 1) * CH)
                        for t in range(CT):
                            dve.scalar_tensor_tensor(out=g[:, t, cols], in0=g[:, t, cols], scalar=pvec[:, t, 1:2],
                                                     in1=rn[0:CP, cols], op0=ALU.mult, op1=ALU.mult).then_inc(ln_op, 1)
                        for t in range(CT):
                            dve.wait_ge(ln_op, LN * b + 4 * c + 1 + t)
                            dve.tensor_scalar(g[:, t, cols], g[:, t, cols], pvec[:, t, 2:3], None, ALU.add).then_inc(ln_op, 1)
                        if c > 0:
                            copies(c - 1)
                    copies(NCH - 1)

                    def take_scores(row, s):
                        for c in range(NQ):
                            dve.wait_ge(s_full, b * USE + PRO + NQ * row + c + 1)
                            if b or not isinstance(row, int) or row:
                                dve.wait_ge(exped, NQ * (RB * b + row - 1) + c + 1)
                            dve.tensor_scalar(vb[:, c * QB:(c + 1) * QB], ps_s[:, c % 2, :], 1.0, None, ALU.mult, ALU.max,
                                              accum_out=mx[:, s, c:c + 1]).then_inc(s_free, 1)
                        dve.wait_ge(s_free, b * USE + PRO + NQ * row + NQ + 2)
                        dve.tensor_reduce(nbias[:, s:s + 1], mx[:, s, :], AX_X, ALU.max, negate=True).then_inc(mx_op, 1)
                        dve.wait_ge(mx_op, 2 * (RB * b + row) + 1)
                        dve.tensor_scalar(nbias[:, s:s + 1], nbias[:, s:s + 1], mix[:, 6:7], None, ALU.mult).then_inc(mx_op, 1)

                    def attention_weights(row, s):
                        for c in range(NQ):
                            cols = slice(c * QB, (c + 1) * QB)
                            dve.scalar_tensor_tensor(out=rn[:, cols], in0=vb[:, cols], scalar=0.0, in1=vb[:, cols],
                                                     op0=ALU.max, op1=ALU.mult).then_inc(r_op, 1)
                        dve.wait_ge(exped, NQ * (RB * b + row) + NQ)
                        dve.tensor_reduce(coef[:, s:s + 1], sums[:, s, :], AX_X, ALU.add).then_inc(c_op, 1)
                        dve.wait_ge(c_op, 3 * (RB * b + row) + 1)
                        dve.reciprocal(coef[:, s:s + 1], coef[:, s:s + 1]).then_inc(c_op, 1)
                        dve.wait_ge(c_op, 3 * (RB * b + row) + 2)
                        dve.tensor_scalar(coef[:, s:s + 1], coef[:, s:s + 1], mix[:, 4:5], None, ALU.mult).then_inc(c_op, 1)
                        dve.wait_ge(c_op, 3 * (RB * b + row) + 3)
                        dve.wait_ge(r_op, NQ * (RB * b + row) + NQ)
                        dve.scalar_tensor_tensor(out=prob[s], in0=prob[s], scalar=coef[:, s:s + 1], in1=rn[:, :],
                                                 op0=ALU.mult, op1=ALU.add).then_inc(p_made, 1)

                    def copy_output(row):
                        dve.wait_ge(w_done, 4 + NG * (RB * b + row) + NG)
                        dve.tensor_copy(ob[:, :], ps_o[:, 0:C]).then_inc(ob_made, 1)

                    def add_output(row, s):
                        dve.wait_ge(f_full, (2 + RB) * b + 2 + row + 1)
                        dve.wait_ge(ot_stored, RB * b + row + 1)
                        cols = bass.ds(row * P, P)
                        dve.tensor_tensor(ot[:, s, :, :], ps_f[0:CP, 0:CT * P].rearrange("p (t n) -> p t n", t=CT),
                                          xg[:, :, cols], ALU.add).then_inc(ot_made, 1)

                    take_scores(0, 0)
                    attention_weights(0, 0)
                    take_scores(1, 1)
                    attention_weights(1, 1)
                    copy_output(0)
                    with dve.Fori(0, RB // 2 - 1) as r:
                        take_scores(2 * r + 2, 0)
                        add_output(2 * r, 0)
                        attention_weights(2 * r + 2, 0)
                        copy_output(2 * r + 1)
                        take_scores(2 * r + 3, 1)
                        add_output(2 * r + 1, 1)
                        attention_weights(2 * r + 3, 1)
                        copy_output(2 * r + 2)
                    add_output(RB - 2, 0)
                    copy_output(RB - 1)
                    add_output(RB - 1, 1)


TILE_BLOCKS = [(0, 4), (8, 9), (1, 5), (2, 6), (10, 11), (3, 7)]


def build(nc, a, out):
    consts = {k: a[k] for k in ("group", "mean", "ident", "ones_blk", "den_sel")}
    z_dram = nc.dram_tensor("z_scratch", [B, C, N], F32, kind="Internal").ap()
    ss_dram = nc.dram_tensor("ss_scratch", [2, N], F32, kind="Internal").ap()
    rn_dram = nc.dram_tensor("rn_scratch", [2, N], F32, kind="Internal").ap()
    o_dram = nc.dram_tensor("o_scratch", [B * HEADS, HD, N], F32, kind="Internal").ap()
    m_dram = nc.dram_tensor("m_scratch", [1, N], F32, kind="Internal").ap()
    r_dram = nc.dram_tensor("r_scratch", [1, N], F32, kind="Internal").ap()
    group_norm_and_store(nc, a["x"], consts, z_dram)
    layer0(nc, z_dram, a["w_qkv"], a["vecs"], a["temperature"], consts, ss_dram, rn_dram, o_dram)
    o_by_image = o_dram.rearrange("(b h) d n -> b (h d) n", b=B)
    layer1(nc, a["x"], o_by_image, {k: a[k] for k in ("wp", "wq", "wk", "wv", "pvec", "mix")}, consts, m_dram, r_dram, out)


def kernel(x, L0_conv_w_qkv, L0_conv_b_qkv, L0_conv_w_dw, L0_conv_b_dw, L0_conv_w_proj, L0_conv_b_proj,
           L0_conv_temperature, L1_conv_ln_w, L1_conv_ln_b, L1_conv_Wq, L1_conv_Wk, L1_conv_Wv, L1_conv_w1, L1_conv_w2):
    import numpy as np
    import concourse.bacc as bacc
    from concourse.bass_utils import run_bass_kernel_spmd

    order = [block for pair in TILE_BLOCKS for block in pair]

    def by_tile(w):
        t = np.asarray(w).reshape(12, HD, -1)[order].reshape(6, 2, HD, -1)
        return np.concatenate([t, t])

    def transposed(w):
        return np.ascontiguousarray(np.asarray(w).T.reshape(CT, CP, -1).transpose(1, 0, 2))

    def channels(v):
        return np.asarray(v).reshape(CT, CP).T

    w_qkv = by_tile(L0_conv_w_qkv).reshape(12, 2, HD, CT, CP).transpose(0, 4, 3, 1, 2)
    vecs = np.concatenate([by_tile(L0_conv_b_qkv), by_tile(L0_conv_w_dw), by_tile(L0_conv_b_dw)], axis=3)
    temperature = np.asarray(L0_conv_temperature).reshape(1, HEADS)

    f = np.float32
    ch = np.arange(CP)
    rows = np.arange(P)
    block_of = np.where(rows % HALF < HD, rows // HALF, -1)
    inputs = {
        "x": np.asarray(x).reshape(B, C, N),
        "w_qkv": w_qkv,
        "vecs": vecs,
        "temperature": np.concatenate([temperature, temperature], axis=1),
        "wp": transposed(L0_conv_w_proj),
        "wq": transposed(L1_conv_Wq),
        "wk": transposed(L1_conv_Wk),
        "wv": transposed(L1_conv_Wv),
        "pvec": np.stack([channels(L0_conv_b_proj), channels(L1_conv_ln_w), channels(L1_conv_ln_b)], axis=2),
        "mix": np.concatenate([np.asarray(L1_conv_w1), np.asarray(L1_conv_w2)]).reshape(1, 2),
        "group": ((ch[:, None] // 6 == ch[None, :] // 6) / 6.0).astype(f),
        "mean": np.full((CP, CP), 1.0 / C, f),
        "ident": np.eye(P, dtype=f),
        "ones_blk": ((block_of[:, None] == block_of[None, :]) & (block_of[:, None] >= 0)).astype(f),
        "den_sel": (rows[:, None] == (rows[None, :] // HALF) * HALF + HD).astype(f),
    }
    nc = bacc.Bacc("TRN2", target_bir_lowering=False, num_devices=1)
    arrays, aps = {}, {}
    for name, value in inputs.items():
        value = np.ascontiguousarray(value)
        arrays[f"in_{name}"] = value
        aps[name] = nc.dram_tensor(f"in_{name}", value.shape, mybir.dt.from_np(value.dtype), kind="ExternalInput").ap()
    out = nc.dram_tensor("out", [B, C, N], F32, kind="ExternalOutput").ap()
    build(nc, aps, out)
    result = run_bass_kernel_spmd(nc, [arrays], core_ids=[0])
    return result.results[0]["out"].reshape(B, C, HH, WW)
```

```python
from contextlib import ExitStack

import concourse.bass as bass
from concourse import mybir

F32 = mybir.dt.float32
F16 = mybir.dt.float16
F32R = mybir.dt.float32r
ALU = mybir.AluOpType
ACT = mybir.ActivationFunctionType
AX_X = mybir.AxisListType.X

B, C, HH, WW = 2, 192, 64, 64
N = HH * WW
HEADS, HD = 4, 48
CT, CP = 2, 96
P = 128
HALF = 64
KR = HALF + HD
CH = 512
NCH = N // CH
KT = N // P
NB = 1024
NBL = N // NB
ROWS = CH // WW
TAPS = 9
PW = WW + 2
SPLIT = 4096.0
SAFE = 60.0

TILES_PAIR = 3
PAIRS = B * HEADS // 2
CONV_OPS = 2 * TAPS

USE_FIRST = 8 + 8 + 8 + 8
USE_EVEN = 8 + 8 + 8 + 4
USE_ODD = 8 + 8 + 8 + 8 + 4
USE_PAIR = USE_EVEN + USE_ODD
DEN_AT = {1: 12, 2: 4, 3: 4}


def group_norm_and_store(nc, x, consts, z_dram):
    with ExitStack() as ctx:
        def sb(name, shape, dt=F32):
            return ctx.enter_context(nc.sbuf_tensor(name, shape, dt))

        def sem(name):
            return ctx.enter_context(nc.semaphore(name))

        NT = B * CT
        xin = sb("gn_x", [CP, NT, N])
        group = sb("gn_group", [CP, CP])
        stats = sb("gn_stats", [CP, NT, NCH, 6])
        mv = sb("gn_mv", [CP, NT, 2])
        mean = sb("gn_mean", [CP, NT])
        dev = sb("gn_dev", [CP, NT])
        var = sb("gn_var", [CP, NT])
        half = sb("gn_half", [CP, NT])
        y = sb("gn_y", [CP, NT])
        t = sb("gn_t", [CP, NT])
        ps = ctx.enter_context(nc.psum_tensor("gn_ps", [P, 2, CH], F32))
        x_in = [sem(f"gn_x_in{i}") for i in range(NT)]
        group_in = sem("gn_group_in")
        vec = sem("gn_vec")
        asked = sem("gn_asked")
        summed = sem("gn_summed")
        pow_asked = sem("gn_pow_asked")
        powed = sem("gn_powed")
        z_made = sem("gn_z_made")
        z_out = sem("gn_z_out")

        with nc.Block() as block:
            @block.sync
            def _(sp):
                for i in range(NT):
                    sp.dma_start(xin[:, i, :], x[i // CT, (i % CT) * CP:(i % CT + 1) * CP, :]).then_inc(x_in[i], 16)
                    if i == 0:
                        sp.dma_start(group[:, :], consts["group"]).then_inc(group_in, 16)
                for i in range(NT):
                    sp.wait_ge(z_made, i + 1)
                    sp.dma_start(z_dram[i // CT, (i % CT) * CP:(i % CT + 1) * CP, :], xin[:, i, :]).then_inc(z_out, 16)
                sp.wait_ge(z_out, 16 * NT)

            @block.gpsimd
            def _(pool):
                pool.memset(half[:, :], -0.5).then_inc(powed, 1)
                pool.wait_ge(powed, 1)
                pool.wait_ge(pow_asked, 1)
                pool.tensor_tensor(y[:, :], var[:, :], half[:, :], ALU.pow).then_inc(powed, 1)

            @block.tensor
            def _(pe):
                pe.wait_ge(group_in, 16)
                for k, src in enumerate((mean, var)):
                    pe.wait_ge(asked, k + 1)
                    pe.matmul(ps[0:CP, k, 0:NT], group[:, :], src[:, :], start=True, stop=True).then_inc(summed, 1)

            @block.vector
            def _(dve):
                n = [0]

                def link(ins):
                    n[0] += 1
                    ins.then_inc(vec, 1)
                    dve.wait_ge(vec, n[0])

                for i in range(NT):
                    dve.wait_ge(x_in[i], 16)
                    for c in range(NCH):
                        ins = dve.bn_stats(stats[:, i, c, :], xin[:, i, c * CH:(c + 1) * CH])
                    link(ins)
                    link(dve.bn_aggr(mv[:, i, :], stats[:, i, :, :].rearrange("p c s -> p (c s)")))
                dve.tensor_copy(mean[:, :], mv[:, :, 0]).then_inc(asked, 1)
                dve.wait_ge(summed, 1)
                dve.wait_ge(asked, 1)
                link(dve.tensor_tensor(dev[:, :], mean[:, :], ps[0:CP, 0, 0:NT], ALU.subtract))
                link(dve.tensor_copy(mean[:, :], ps[0:CP, 0, 0:NT]))
                link(dve.tensor_tensor(dev[:, :], dev[:, :], dev[:, :], ALU.mult))
                dve.tensor_tensor(var[:, :], mv[:, :, 1], dev[:, :], ALU.add).then_inc(asked, 1)
                dve.wait_ge(summed, 2)
                dve.wait_ge(asked, 2)
                dve.tensor_scalar(var[:, :], ps[0:CP, 1, 0:NT], 1e-5, None, ALU.add).then_inc(pow_asked, 1)
                dve.wait_ge(powed, 2)
                dve.wait_ge(pow_asked, 1)
                link(dve.scalar_tensor_tensor(out=t[:, :], in0=var[:, :], scalar=-0.5, in1=y[:, :], op0=ALU.mult, op1=ALU.mult))
                link(dve.tensor_tensor(t[:, :], t[:, :], y[:, :], ALU.mult))
                link(dve.scalar_tensor_tensor(out=y[:, :], in0=t[:, :], scalar=1.5, in1=y[:, :], op0=ALU.add, op1=ALU.mult))
                for i in range(NT):
                    dve.tensor_scalar(xin[:, i, :], xin[:, i, :], mean[:, i:i + 1], y[:, i:i + 1],
                                      ALU.subtract, ALU.mult).then_inc(z_made, 1)


class Uses:

    def __init__(self, base):
        self.base, self.n = base, 0

    def next(self):
        self.n += 1
        return self.base + self.n - 1, (self.n - 1) % 2


def layer0(nc, z_dram, w_qkv, vecs, temperature, consts, ss_dram, rn_dram, o_dram):
    with ExitStack() as ctx:
        def sb(name, shape, dt=F32):
            return ctx.enter_context(nc.sbuf_tensor(name, shape, dt))

        def psum(name, shape):
            return ctx.enter_context(nc.psum_tensor(name, shape, F32))

        def sem(name):
            return ctx.enter_context(nc.semaphore(name))

        ZS = 4
        z = sb("z", [CP, ZS, CT, CH])
        w = sb("w", [CP, TILES_PAIR, CT, P])
        vec = sb("vec", [P, TILES_PAIR, TAPS + 2])
        pad = sb("pad", [KR, PW, PW])
        qk = sb("qk", [KR, N])
        vv = sb("vv", [KR, N])
        sq = sb("sq", [KR, N])
        ss = sb("ss", [KR, N])
        nrm = sb("nrm", [P, 2, KT])
        nry = sb("nry", [P, 2, KT])
        nrt = sb("nrt", [P, 2, KT])
        mhalf = sb("mhalf", [P, 2, KT])
        u = sb("u", [KR, NB])
        hi = sb("hi", [KR, 2, NB], F16)
        lo = sb("lo", [KR, 2, NB], F16)
        q_hi = sb("q_hi", [KR, 2, N], F16)
        q_lo = sb("q_lo", [KR, 2, N], F16)
        k_hl = sb("k_hl", [KR, 2, N], F16)
        vt = sb("vt", [P, 2, KT, HALF])
        prob = sb("prob", [P, 2, NB])
        acc_s = sb("acc_s", [P, CH])
        rden = sb("rden", [P, CH])
        o_s = sb("o_s", [P, 2, CH])
        ident = sb("ident", [P, P])
        ones_blk = sb("ones_blk", [P, P])
        den_sel = sb("den_sel", [P, P])
        temp = sb("temp", [P, B * HEADS])
        tabs = sb("tabs", [P, B * HEADS])
        cur = sb("cur", [P, 2, 2])

        ps_s = psum("ps_s", [P, 2, NB])
        ps_a = psum("ps_a", [P, 2, CH])
        ps_h = psum("ps_h", [P, 2, CH])

        z_in = [sem(f"z_in{i}") for i in range(ZS)]
        w_in = [sem(f"w_in{i}") for i in range(TILES_PAIR)]
        const_in = sem("const_in")
        help_full = sem("help_full")
        help_free = sem("help_free")
        conv_op = sem("conv_op")
        sq_done = sem("sq_done")
        ss_out = sem("ss_out")
        ss_in = sem("ss_in")
        norm_asked = sem("norm_asked")
        powed = sem("powed")
        norm_op = sem("norm_op")
        rn_out = sem("rn_out")
        rn_in = sem("rn_in")
        unit_op = sem("unit_op")
        lo_done = sem("lo_done")
        split_in = [sem(f"split_in{i}") for i in range(2)]
        cur_set = sem("cur_set")
        scores = sem("scores")
        exped = sem("exped")
        pv_done = sem("pv_done")
        acc_free = sem("acc_free")
        o_op = sem("o_op")
        o_out = sem("o_out")
        o_stored = sem("o_stored")
        zero_set = sem("zero_set")
        vt_set = sem("vt_set")
        temp_op = sem("temp_op")

        STEPS = NBL * KT
        NCONST = 4

        with nc.Block() as block:
            @block.sync
            def _(sp):
                sp.dma_start(ident[:, :], consts["ident"]).then_inc(const_in, 16)
                sp.dma_start(ones_blk[:, :], consts["ones_blk"]).then_inc(const_in, 16)
                sp.dma_start(den_sel[:, :], consts["den_sel"]).then_inc(const_in, 16)
                sp.dma_start(temp[:, :], temperature.partition_broadcast(P)).then_inc(const_in, 16)

                def load_w(slot, tile):
                    sp.dma_start(w[:, slot, :, :].rearrange("p c (h o) -> p c h o", h=2)[:, :, :, 0:HD],
                                 w_qkv[tile]).then_inc(w_in[slot], 16)
                    for h in range(2):
                        sp.dma_start(vec[h * HALF:h * HALF + HD, slot, :], vecs[tile, h]).then_inc(w_in[slot], 16)

                def load_z(chunks, batch, taken):
                    for c in chunks:
                        if taken is not None:
                            sp.wait_ge(help_full, taken + c % ZS)
                        sp.dma_start(z[:, c % ZS, :, :],
                                     z_dram[batch, :, c * CH:(c + 1) * CH].rearrange("(t p) n -> p t n", p=CP)
                                     ).then_inc(z_in[c % ZS], 16)

                def store_block(g, j):
                    sp.wait_ge(o_op, NBL * g + j + 2)
                    for h in range(2):
                        sp.dma_start(o_dram[g, :, j * NB + h * CH:j * NB + (h + 1) * CH],
                                     o_s[h * HALF:h * HALF + HD, j % 2, :]).then_inc(o_out, 16)
                    sp.wait_ge(o_out, 32 * (NBL * g + j + 1))
                    sp.sem_inc(o_stored, 1)

                def sums_out(free_needed, k):
                    sp.wait_ge(help_free, free_needed)
                    for h in range(2):
                        sp.dma_start(ss_dram[h:h + 1, :], ss[h * HALF:h * HALF + 1, :]).then_inc(ss_out, 16)
                    sp.wait_ge(ss_out, 32 * k + 32)
                    sp.dma_start(nrm[:, :, :], ss_dram.rearrange("h (p t) -> p h t", p=P)).then_inc(ss_in, 16)

                def norms_out(k):
                    sp.wait_ge(norm_op, 4 * k + 4)
                    sp.dma_start(rn_dram.rearrange("h (p t) -> p h t", p=P), nry[:, :, :]).then_inc(rn_out, 16)
                    sp.wait_ge(rn_out, 16 * k + 16)
                    for h in range(2):
                        sp.dma_start(sq[h * HALF:h * HALF + HD, :],
                                     rn_dram[h:h + 1, :].partition_broadcast(HD)).then_inc(rn_in, 16)

                def split_out(slot, k, scores_needed):
                    if scores_needed is not None:
                        sp.wait_ge(scores, scores_needed)
                    for c in range(4):
                        cols = slice(c * NB, (c + 1) * NB)
                        sp.wait_ge(unit_op, 8 * k + 2 * c + 2)
                        for dst, src in ((q_hi[0:HD], hi[0:HD]), (q_hi[HALF:KR], hi[0:HD]), (k_hl[0:HD], hi[HALF:KR])):
                            sp.dma_start(dst[:, slot, cols], src[:, c % 2, :]).then_inc(split_in[c % 2], 16)
                        sp.wait_ge(lo_done, 4 * k + c + 1)
                        for dst, src in ((q_lo[0:HD], lo[0:HD]), (q_lo[HALF:KR], lo[0:HD]), (k_hl[HALF:KR], lo[HALF:KR])):
                            sp.dma_start(dst[:, slot, cols], src[:, c % 2, :]).then_inc(split_in[c % 2], 16)

                sp.sem_inc(o_stored, 2)
                sp.wait_ge(zero_set, 1)
                for t in range(TILES_PAIR):
                    load_w(t, t)
                load_z(range(4), 0, None)
                load_z(range(4, 8), 0, 1)
                load_z(range(4), 0, 5)
                sums_out(16, 0)
                load_z(range(4, 8), 0, 17)
                norms_out(0)
                sp.wait_ge(zero_set, 3)
                split_out(0, 0, None)

                def pair(i, last):
                    base, g = USE_FIRST + i * USE_PAIR, 2 * i
                    if not last:
                        sp.wait_ge(conv_op, CONV_OPS * (3 * i + 2))
                        for t in range(2):
                            load_w(t, 3 * i + 3 + t)
                    load_z(range(4), i // 2, base - 11)
                    load_z(range(4, 8), i // 2, base + 1)
                    store_block(g, 0)
                    sums_out(base + 17, g + 1)
                    store_block(g, 1)
                    norms_out(g + 1)
                    split_out(1, g + 1, STEPS * g + 1)
                    store_block(g, 2)
                    store_block(g, 3)
                    base, g = base + USE_EVEN, g + 1
                    if not last:
                        sp.wait_ge(conv_op, CONV_OPS * (3 * i + 3))
                        load_w(2, 3 * i + 5)
                        nxt = (i + 1) // 2
                        load_z(range(4), nxt, base)
                        load_z(range(4, 8), nxt, base + 1)
                        load_z(range(4), nxt, base + 5)
                    store_block(g, 0)
                    if not last:
                        sums_out(base + 17, g + 1)
                        load_z(range(4, 8), nxt, base + 18)
                    store_block(g, 1)
                    if not last:
                        norms_out(g + 1)
                        split_out(0, g + 1, STEPS * g + 1)
                    store_block(g, 2)
                    store_block(g, 3)

                with sp.Fori(0, PAIRS - 1) as i:
                    pair(i, False)
                pair(PAIRS - 1, True)

            @block.gpsimd
            def _(pool):
                pool.memset(w[:, :, :, :], 0.0)
                pool.memset(vec[:, :, :], 0.0).then_inc(zero_set, 1)
                pool.memset(pad[:, :, :], 0.0).then_inc(zero_set, 1)
                pool.memset(q_hi[:, :, :], 0.0)
                pool.memset(q_lo[:, :, :], 0.0)
                pool.memset(k_hl[:, :, :], 0.0).then_inc(zero_set, 1)
                pool.memset(mhalf[:, :, :], -0.5).then_inc(zero_set, 1)
                pool.memset(vt[:, :, :, HD:HALF], 0.0).then_inc(vt_set, 1)
                pool.wait_ge(vt_set, 1)
                pool.memset(vt[:, :, :, HD:HD + 1], 1.0).then_inc(vt_set, 1)

                def prepare(k, convs):
                    pool.wait_ge(conv_op, CONV_OPS * convs)
                    for c in range(4):
                        cols = slice(c * NB, (c + 1) * NB)
                        pool.tensor_tensor(sq[:, cols], qk[:, cols], qk[:, cols], ALU.mult).then_inc(sq_done, 1)
                    pool.wait_ge(norm_asked, k + 1)
                    pool.tensor_tensor(nry[:, :, :], nrm[:, :, :], mhalf[:, :, :], ALU.pow).then_inc(powed, 1)
                    for c in range(4):
                        pool.wait_ge(unit_op, 8 * k + 2 * c + 2)
                        pool.tensor_tensor(lo[:, c % 2, :], u[:, :], hi[:, c % 2, :], ALU.subtract).then_inc(lo_done, 1)

                pool.wait_ge(zero_set, 4)
                prepare(0, 1)

                def pair(i, last):
                    prepare(2 * i + 1, 3 * i + 3)
                    if not last:
                        prepare(2 * i + 2, 3 * i + 4)

                with pool.Fori(0, PAIRS - 1) as i:
                    pair(i, False)
                pair(PAIRS - 1, True)

            @block.scalar
            def _(act):
                def head(slot, g):
                    act.wait_ge(cur_set, g + 1)
                    for a in range(STEPS):
                        act.wait_ge(scores, STEPS * g + a + 1)
                        if a >= 2 or not isinstance(g, int) or g > 0:
                            act.wait_ge(pv_done, STEPS * g + a - 1)
                        act.activation(prob[:, a % 2, :], ps_s[:, a % 2, :], ACT.Exp,
                                       bias=cur[:, slot, 1:2], scale=cur[:, slot, 0:1]).then_inc(exped, 1)

                act.sem_inc(exped, 2)
                head(0, 0)
                with act.Fori(0, PAIRS - 1) as i:
                    head(1, 2 * i + 1)
                    head(0, 2 * i + 2)
                head(1, 2 * PAIRS - 1)

            @block.tensor
            def _(pe):
                def project(slot, tile, c, use):
                    n, bank = use
                    helper_free(n)
                    pe.wait_ge(z_in[c % ZS], 16 * (2 * tile + c // ZS + 1))
                    for t in range(CT):
                        ins = pe.matmul(ps_h[0:KR, bank, :], w[:, slot, t, 0:KR], z[:, c % ZS, t, :],
                                        start=(t == 0), stop=(t == CT - 1))
                    ins.then_inc(help_full, 1)

                def helper_free(n):
                    if not isinstance(n, int) or n >= 2:
                        pe.wait_ge(help_free, n - 1)

                def sums(c, k, use):
                    n, bank = use
                    helper_free(n)
                    pe.wait_ge(sq_done, 4 * k + c // 2 + 1)
                    pe.matmul(ps_h[0:KR, bank, :], ones_blk[0:KR, 0:KR], sq[:, c * CH:(c + 1) * CH],
                              start=True, stop=True).then_inc(help_full, 1)

                def transpose_v(q, use):
                    n, bank = use
                    helper_free(n)
                    for m4 in range(4):
                        m = q * 4 + m4
                        ins = pe.transpose(ps_h[:, bank, m4 * P:m4 * P + KR], vv[:, m * P:(m + 1) * P], ident[0:KR, 0:KR])
                    ins.then_inc(help_full, 1)

                def denominators(g, j, use):
                    n, bank = use
                    helper_free(n)
                    pe.wait_ge(acc_free, NBL * g + j + 3)
                    pe.matmul(ps_h[:, bank, :], den_sel[:, :], acc_s[:, :], start=True, stop=True).then_inc(help_full, 1)

                uses = Uses(0)
                pe.wait_ge(const_in, 16 * NCONST)
                pe.wait_ge(w_in[0], 48)
                for c in range(8):
                    project(0, 0, c, uses.next())
                for c in range(8):
                    sums(c, 0, uses.next())
                pe.wait_ge(w_in[1], 48)
                for c in range(8):
                    project(1, 1, c, uses.next())
                pe.wait_ge(conv_op, CONV_OPS * 2)
                for q in range(8):
                    transpose_v(q, uses.next())

                def head(slot, g, base, late, prep):
                    uses = Uses(base)
                    pe.wait_ge(help_free, base - late)
                    for c in range(2):
                        pe.wait_ge(split_in[c], 96 * 2 * (g + 1))

                    def score(a):
                        j, m = a // KT, a % KT
                        pe.wait_ge(exped, STEPS * g + a + 1)
                        for h in range(2):
                            cols = slice(j * NB + h * CH, j * NB + (h + 1) * CH)
                            for t, q in enumerate((q_hi, q_lo)):
                                ins = pe.matmul(ps_s[:, a % 2, h * CH:(h + 1) * CH], k_hl[:, slot, m * P:(m + 1) * P],
                                                q[:, slot, cols], start=(t == 0), stop=(t == 1))
                        ins.then_inc(scores, 1)

                    def weigh(a):
                        j, m = a // KT, a % KT
                        pe.wait_ge(exped, STEPS * g + a + 3)
                        if m == 0:
                            pe.wait_ge(acc_free, NBL * g + j + 1)
                        for h in range(2):
                            ins = pe.matmul(ps_a[h * HALF:(h + 1) * HALF, j % 2, :], vt[:, slot, m, :],
                                            prob[:, a % 2, h * CH:(h + 1) * CH], start=(m == 0), stop=(m == KT - 1))
                        ins.then_inc(pv_done, 1)

                    score(0)
                    for a in range(STEPS):
                        j, m = a // KT, a % KT
                        if a + 1 < STEPS:
                            score(a + 1)
                        weigh(a)
                        prep(j, m, uses)
                        if j >= 1 and m == DEN_AT[j]:
                            denominators(g, j - 1, uses.next())
                    denominators(g, NBL - 1, uses.next())

                def even(i):
                    def prep(j, m, uses):
                        if j == 0 and m in range(3, 19, 2):
                            if m == 3:
                                pe.wait_ge(w_in[2], 48 * (i + 1))
                            project(2, 3 * i + 2, (m - 3) // 2, uses.next())
                        if j == 1 and m in range(14, 30, 2):
                            sums((m - 14) // 2, 2 * i + 1, uses.next())
                        if j == 3 and m in range(8, 24, 2):
                            transpose_v((m - 8) // 2, uses.next())
                    head(0, 2 * i, USE_FIRST + i * USE_PAIR, 0, prep)

                def odd(i, last):
                    def prep(j, m, uses):
                        if last:
                            return
                        if j == 0 and m in range(3, 19, 2):
                            if m == 3:
                                pe.wait_ge(w_in[0], 48 * (i + 2))
                            project(0, 3 * i + 3, (m - 3) // 2, uses.next())
                        if j == 1 and m in range(14, 22):
                            sums(m - 14, 2 * i + 2, uses.next())
                        if j == 1 and m in range(22, 30):
                            if m == 22:
                                pe.wait_ge(w_in[1], 48 * (i + 2))
                            project(1, 3 * i + 4, m - 22, uses.next())
                        if j == 3 and m in range(16, 32, 2):
                            if m == 16:
                                pe.wait_ge(conv_op, CONV_OPS * (3 * i + 5))
                            transpose_v((m - 16) // 2, uses.next())
                    head(1, 2 * i + 1, USE_FIRST + i * USE_PAIR + USE_EVEN, 1, prep)

                with pe.Fori(0, PAIRS - 1) as i:
                    even(i)
                    odd(i, False)
                even(PAIRS - 1)
                odd(PAIRS - 1, True)

            @block.vector
            def _(dve):
                def full(n):
                    dve.wait_ge(help_full, n + 1)

                def evac_project(slot, c, use):
                    n, bank = use
                    full(n)
                    rows = slice(1 + c * ROWS, 1 + (c + 1) * ROWS)
                    dve.tensor_scalar(pad[:, rows, 1:WW + 1], ps_h[0:KR, bank, :].rearrange("p (r c) -> p r c", c=WW),
                                      vec[0:KR, slot, 0:1], None, ALU.add).then_inc(help_free, 1)

                def conv(slot, dst, tiles, n_free):
                    dve.wait_ge(help_free, n_free)
                    for tap in range(TAPS):
                        dy, dx = tap // 3, tap % 3
                        for h in range(2):
                            r0 = h * (HH // 2)
                            src = pad[:, r0 + dy:r0 + dy + HH // 2, dx:dx + WW]
                            out = dst[:, h * N // 2:(h + 1) * N // 2].rearrange("p (r c) -> p r c", c=WW)
                            if tap == 0:
                                ins = dve.tensor_scalar(out, src, vec[0:KR, slot, 1:2], vec[0:KR, slot, 10:11],
                                                        ALU.mult, ALU.add)
                            else:
                                dve.wait_ge(conv_op, CONV_OPS * tiles + 2 * tap + h - 1)
                                ins = dve.scalar_tensor_tensor(out=out, in0=src, scalar=vec[0:KR, slot, 1 + tap:2 + tap],
                                                               in1=out, op0=ALU.mult, op1=ALU.add)
                            ins.then_inc(conv_op, 1)

                def evac_sums(c, use):
                    n, bank = use
                    full(n)
                    dve.tensor_copy(ss[:, c * CH:(c + 1) * CH], ps_h[0:KR, bank, :]).then_inc(help_free, 1)

                def norms(k):
                    dve.wait_ge(ss_in, 16 * k + 16)
                    if not (isinstance(k, int) and k == 0):
                        dve.wait_ge(rn_out, 16 * k)
                    dve.tensor_scalar(nrm[:, :, :], nrm[:, :, :], 1e-24, None, ALU.max).then_inc(norm_asked, 1)
                    dve.wait_ge(norm_asked, k + 1)
                    dve.wait_ge(powed, k + 1)
                    dve.scalar_tensor_tensor(out=nrt[:, :, :], in0=nrm[:, :, :], scalar=-0.5, in1=nry[:, :, :],
                                             op0=ALU.mult, op1=ALU.mult).then_inc(norm_op, 1)
                    dve.wait_ge(norm_op, 4 * k + 1)
                    dve.tensor_tensor(nrt[:, :, :], nrt[:, :, :], nry[:, :, :], ALU.mult).then_inc(norm_op, 1)
                    dve.wait_ge(norm_op, 4 * k + 2)
                    dve.scalar_tensor_tensor(out=nry[:, :, :], in0=nrt[:, :, :], scalar=1.5, in1=nry[:, :, :],
                                             op0=ALU.add, op1=ALU.mult).then_inc(norm_op, 1)
                    dve.wait_ge(norm_op, 4 * k + 3)
                    dve.tensor_scalar(nry[:, :, :], nry[:, :, :], SPLIT, None, ALU.mult).then_inc(norm_op, 1)

                def split(k):
                    dve.wait_ge(rn_in, 32 * k + 32)
                    for c in range(4):
                        cols = slice(c * NB, (c + 1) * NB)
                        if c >= 1:
                            dve.wait_ge(lo_done, 4 * k + c)
                        elif not (isinstance(k, int) and k == 0):
                            dve.wait_ge(lo_done, 4 * k)
                        for h in range(2):
                            r = slice(h * HALF, h * HALF + HD)
                            ins = dve.tensor_tensor(u[r, :], qk[r, cols], sq[r, cols], ALU.mult)
                        ins.then_inc(unit_op, 1)
                        dve.wait_ge(unit_op, 8 * k + 2 * c + 1)
                        if c >= 2 or not (isinstance(k, int) and k == 0):
                            dve.wait_ge(split_in[c % 2], 96 * (2 * k + c // 2))
                        dve.tensor_copy(hi[:, c % 2, :], u[:, :]).then_inc(unit_op, 1)

                def evac_vt(slot, q, use):
                    n, bank = use
                    full(n)
                    dve.tensor_copy(vt[:, slot, q * 4:(q + 1) * 4, 0:HD],
                                    ps_h[:, bank, :].rearrange("p (m d) -> p m d", d=P)[:, :, slot * HALF:slot * HALF + HD]
                                    ).then_inc(help_free, 1)

                def set_cur(slot, g):
                    dve.wait_ge(temp_op, 4)
                    if not (isinstance(g, int) and g == 0):
                        dve.wait_ge(exped, STEPS * (g - 1) + 3)
                    dve.tensor_copy(cur[:, slot, 0:1], temp[:, bass.ds(g, 1)])
                    dve.tensor_copy(cur[:, slot, 1:2], tabs[:, bass.ds(g, 1)]).then_inc(cur_set, 1)

                def copy_acc(g, j):
                    dve.wait_ge(pv_done, STEPS * g + KT * (j + 1))
                    dve.wait_ge(o_op, NBL * g + j + 1)
                    dve.tensor_copy(acc_s[:, :], ps_a[:, j % 2, :]).then_inc(acc_free, 1)

                def finish(g, j, use):
                    n, bank = use
                    full(n)
                    dve.reciprocal(rden[:, :], ps_h[:, bank, :]).then_inc(help_free, 1)
                    dve.wait_ge(help_free, n + 1)
                    dve.wait_ge(o_stored, NBL * g + j + 1)
                    dve.tensor_tensor(o_s[:, j % 2, :], acc_s[:, :], rden[:, :], ALU.mult).then_inc(o_op, 1)

                dve.sem_inc(acc_free, 2)
                dve.sem_inc(o_op, 1)
                dve.wait_ge(const_in, 16 * NCONST)
                dve.tensor_scalar(tabs[:, :], temp[:, :], -1.0, None, ALU.mult).then_inc(temp_op, 1)
                dve.wait_ge(temp_op, 1)
                dve.tensor_tensor(tabs[:, :], tabs[:, :], temp[:, :], ALU.max).then_inc(temp_op, 1)
                dve.wait_ge(temp_op, 2)
                dve.tensor_scalar(tabs[:, :], tabs[:, :], -1.0, SAFE, ALU.mult, ALU.add).then_inc(temp_op, 1)
                dve.wait_ge(temp_op, 3)
                dve.tensor_scalar(tabs[:, :], tabs[:, :], 0.0, None, ALU.min)
                dve.tensor_scalar(temp[:, :], temp[:, :], 1.0 / (SPLIT * SPLIT), None, ALU.mult).then_inc(temp_op, 1)
                set_cur(0, 0)

                dve.memset(u[:, :], 0.0).then_inc(temp_op, 1)
                dve.wait_ge(temp_op, 5)

                dve.wait_ge(zero_set, 2)
                uses = Uses(0)
                dve.wait_ge(w_in[0], 48)
                for c in range(8):
                    evac_project(0, c, uses.next())
                conv(0, qk, 0, 8)
                for c in range(8):
                    evac_sums(c, uses.next())
                dve.wait_ge(w_in[1], 48)
                for c in range(8):
                    evac_project(1, c, uses.next())
                norms(0)
                conv(1, vv, 1, 24)
                split(0)
                dve.wait_ge(vt_set, 2)
                for q in range(8):
                    evac_vt(0, q, uses.next())

                def even(i):
                    uses = Uses(USE_FIRST + i * USE_PAIR)
                    g = 2 * i
                    set_cur(1, g + 1)
                    dve.wait_ge(w_in[2], 48 * (i + 1))
                    for c in range(8):
                        evac_project(2, c, uses.next())
                    conv(2, qk, 3 * i + 2, uses.base + uses.n)
                    copy_acc(g, 0)
                    finish(g, 0, uses.next())
                    for c in range(8):
                        evac_sums(c, uses.next())
                    copy_acc(g, 1)
                    finish(g, 1, uses.next())
                    norms(g + 1)
                    split(g + 1)
                    copy_acc(g, 2)
                    finish(g, 2, uses.next())
                    dve.wait_ge(pv_done, STEPS * g + 1)
                    for q in range(8):
                        evac_vt(1, q, uses.next())
                    copy_acc(g, 3)
                    finish(g, 3, uses.next())

                def odd(i, last):
                    uses = Uses(USE_FIRST + i * USE_PAIR + USE_EVEN)
                    g = 2 * i + 1
                    if not last:
                        set_cur(0, g + 1)
                        dve.wait_ge(w_in[0], 48 * (i + 2))
                        for c in range(8):
                            evac_project(0, c, uses.next())
                        conv(0, qk, 3 * i + 3, uses.base + uses.n)
                    copy_acc(g, 0)
                    finish(g, 0, uses.next())
                    if not last:
                        for c in range(8):
                            evac_sums(c, uses.next())
                        dve.wait_ge(w_in[1], 48 * (i + 2))
                        for c in range(8):
                            evac_project(1, c, uses.next())
                        v_uses = uses.base + uses.n
                    copy_acc(g, 1)
                    finish(g, 1, uses.next())
                    if not last:
                        norms(g + 1)
                        conv(1, vv, 3 * i + 4, v_uses)
                        split(g + 1)
                    copy_acc(g, 2)
                    finish(g, 2, uses.next())
                    if not last:
                        dve.wait_ge(pv_done, STEPS * g + 1)
                        for q in range(8):
                            evac_vt(0, q, uses.next())
                    copy_acc(g, 3)
                    finish(g, 3, uses.next())

                with dve.Fori(0, PAIRS - 1) as i:
                    even(i)
                    odd(i, False)
                even(PAIRS - 1)
                odd(PAIRS - 1, True)


def layer1(nc, x, o_dram, weights, consts, m_dram, r_dram, res_dram, q_dram, out):
    with ExitStack() as ctx:
        def sb(name, shape, dt=F32, scope=None):
            return (scope or ctx).enter_context(nc.sbuf_tensor(name, shape, dt))

        def psum(name, shape):
            return ctx.enter_context(nc.psum_tensor(name, shape, F32))

        def sem(name):
            return ctx.enter_context(nc.semaphore(name))

        QB = 1024
        NQ = N // QB
        RB = KT
        GR = 4
        NG = KT // GR
        TR = 3
        TU = NG + 1
        PRO = 8 * 3 + 16
        USE = PRO + RB * NQ
        RT = 2 * C // P

        gp = sb("gp", [P, CT, N])
        g = gp[0:CP, :, :]
        prob = [gp[:, s, :] for s in range(2)]
        vb = sb("vb", [P, N])
        rn = sb("rn", [P, N])
        v_hi = sb("v_hi", [P, KT, C], F32R)
        v_lo = sb("v_lo", [P, KT, C], F32R)
        wq = sb("wq", [CP, CT, C])
        wk = sb("wk", [CP, CT, C])
        wqk = sb("wqk", [CP, CT, C])
        wv = sb("wv", [CP, CT, C])
        wp = sb("wp", [CP, CT, C])
        pvec = sb("pvec", [CP, CT, 3])
        mixw = sb("mixw", [P, 2])
        mix = sb("mix", [P, 8])
        mtmp = sb("mtmp", [P, 2])
        group = sb("group1", [CP, CP])
        meanm = sb("meanm", [CP, CP])
        ident = sb("ident1", [P, P])
        stats = sb("stats", [CP, CT, NCH, 6])
        mv = sb("mv", [CP, CT, 2])
        gst = sb("gst", [CP, 5, CT])
        mhalf = sb("mhalf1", [P, KT])
        tv = sb("tv", [P, KT])
        ty = sb("ty", [P, KT])
        tt = sb("tt", [P, KT])
        mx = sb("mx", [P, 2, NQ])
        nbias = sb("nbias", [P, 2])
        sums = sb("sums", [P, 2, NQ])
        coef = sb("coef", [P, 2])
        ob = sb("ob", [P, C])

        with ExitStack() as first:
            xg = sb("xg", [CP, CT, N], F32, first)
            o_buf = sb("o_buf", [CP, 4, CT, CH], F32, first)
            x_buf = sb("x_buf", [CP, 4, CT, CH], F32, first)
            sq_buf = sb("sq_buf", [CP, 2, CT, CH], F32, first)
        kst = sb("kst", [P, RT, N], F32R)
        with ExitStack() as second:
            xs = sb("xs", [CP, 2, 2, CT, CH], F32R, second)
            qst = sb("qst", [CP, 2, 2, CT, CH], F32R, second)
        at_hi = sb("at_hi", [P, 4, GR * P], F32R)
        at_lo = sb("at_lo", [P, 4, GR * P], F32R)
        qs = sb("qs", [P, 2, 2 * RT, P], F32R)
        res = sb("res", [CP, 2, CT, P])
        ot = sb("ot", [CP, 2, CT, P])

        ps_s = psum("ps_s1", [P, 2, QB])
        ps_t = psum("ps_t1", [P, TR, CH])
        ps_o = psum("ps_o1", [P, CH])

        const_in = sem("const_in1")
        chunk_in = [sem(f"chunk_in{i}") for i in range(4)]
        s_full = sem("s_full")
        s_free = sem("s_free")
        stat = sem("stat")
        f_full = sem("f_full")
        wqk_set = sem("wqk_set")
        pow_asked = sem("pow_asked1")
        powed = sem("powed1")
        g_ready = sem("g_ready")
        g_made = sem("g_made")
        xg_made = sem("xg_made")
        res_out = sem("res_out")
        dev_made = sem("dev_made")
        sq_made = sem("sq_made1")
        v_out = sem("v_out")
        v_in = sem("v_in")
        tok = sem("tok")
        r_out = sem("r_out")
        r_in = sem("r_in")
        ln_op = sem("ln_op")
        xh_made = sem("xh_made")
        xl_made = sem("xl_made")
        k_in = [sem(f"k_in{i}") for i in range(2)]
        ph_made = sem("ph_made")
        ql_made = sem("ql_made")
        q_out = [sem(f"q_out{i}") for i in range(2)]
        mix_op = sem("mix_op")
        mix_exp = sem("mix_exp")
        qs_in = [sem(f"qs_in{i}") for i in range(2)]
        mx_op = sem("mx_op")
        relued = sem("relued")
        exped = sem("exped1")
        squared = sem("squared")
        c_op = sem("c_op")
        p_made = sem("p_made")
        t_full = sem("t_full")
        hi_made = sem("hi_made")
        t_free = sem("t_free")
        w_done = sem("w_done")
        ob_made = sem("ob_made")
        res_in = [sem(f"res_in{i}") for i in range(2)]
        ot_out = sem("ot_out")
        ot_stored = sem("ot_stored")

        NCONST = 9
        STAT, TOK, LN = 8, 4, 4 * NCH
        FUSE = 2

        def turn(b, row, j):
            return TU * (RB * b + row) + 1 + j

        with nc.Block() as block:
            @block.sync
            def _(sp):
                for dst, src in ((wp, weights["wp"]), (wq, weights["wq"]), (wk, weights["wk"]), (wv, weights["wv"])):
                    sp.dma_start(dst[:, :, :], src).then_inc(const_in, 16)
                sp.dma_start(pvec[:, :, :], weights["pvec"]).then_inc(const_in, 16)
                sp.dma_start(mixw[:, :], weights["mix"].partition_broadcast(P)).then_inc(const_in, 16)
                sp.dma_start(group[:, :], consts["group"]).then_inc(const_in, 16)
                sp.dma_start(meanm[:, :], consts["mean"]).then_inc(const_in, 16)
                sp.dma_start(ident[:, :], consts["ident"]).then_inc(const_in, 16)
                sp.sem_inc(ot_stored, 2)

                def image(b):
                    if b:
                        sp.wait_ge(w_done, 4 + NG * RB * b)
                    for c in range(NCH):
                        s = c % 4
                        if c >= 4:
                            sp.wait_ge(stat, (STAT + NCH) * b + c - 3)
                        cols = slice(c * CH, (c + 1) * CH)
                        for buf, src in ((o_buf, o_dram[b]), (x_buf, x[b])):
                            sp.dma_start(buf[:, s, :, :],
                                         src[:, cols].rearrange("(t p) n -> p t n", p=CP)).then_inc(chunk_in[s], 16)
                    for c in range(NCH):
                        sp.wait_ge(xg_made, NCH * b + c + 1)
                        cols = slice(c * CH, (c + 1) * CH)
                        sp.dma_start(res_dram[b, :, cols].rearrange("(t p) n -> p t n", p=CP), xg[:, :, cols]).then_inc(res_out, 16)
                    sp.wait_ge(s_free, b * USE + 2 + 24)
                    sp.dma_start(m_dram, vb[0:1, :]).then_inc(v_out, 16)
                    sp.wait_ge(v_out, 16 * b + 16)
                    sp.dma_start(tv[:, :], m_dram.rearrange("o (p t) -> (o p) t", p=P)).then_inc(v_in, 16)
                    sp.wait_ge(tok, TOK * b + 4)
                    sp.dma_start(r_dram.rearrange("o (p t) -> (o p) t", p=P), ty[:, :]).then_inc(r_out, 16)
                    sp.wait_ge(r_out, 16 * b + 16)
                    sp.dma_start(rn[0:CP, :], r_dram.partition_broadcast(CP)).then_inc(r_in, 16)

                    sp.wait_ge(res_out, 16 * NCH * (b + 1))

                    def place_k(c):
                        cols = slice(c * CH, (c + 1) * CH)
                        s = c % 2
                        sp.wait_ge(xh_made, NCH * b + c + 1)
                        for tile, to, part, t, frm, n in ((0, 0, 0, 0, 0, 96), (0, 96, 0, 1, 0, 32), (1, 0, 0, 1, 32, 64),
                                                          (1, 64, 1, 0, 0, 64), (2, 0, 1, 0, 64, 32), (2, 32, 1, 1, 0, 96)):
                            if (tile, to) == (1, 64):
                                sp.wait_ge(xl_made, NCH * b + c + 1)
                            sp.dma_start(kst[to:to + n, tile, cols].bitcast(F32), xs[frm:frm + n, s, part, t, :].bitcast(F32)).then_inc(k_in[s], 16)

                    def store_q(c):
                        cols = slice(c * CH, (c + 1) * CH)
                        s = c % 2
                        sp.wait_ge(ql_made, NCH * b + c + 1)
                        for part in range(2):
                            for copy in range(2):
                                r0 = (2 * part + copy) * C
                                sp.dma_start(q_dram[r0:r0 + C, cols].rearrange("(t p) n -> p t n", p=CP),
                                             qst[:, s, part, :, :].bitcast(F32)).then_inc(q_out[s], 16)

                    for c in range(NCH):
                        place_k(c)
                        if c:
                            store_q(c - 1)
                    store_q(NCH - 1)
                    for s in range(2):
                        sp.wait_ge(q_out[s], 4 * 16 * NCH // 2 * (b + 1))

                    def load_q(row, s):
                        sp.wait_ge(s_full, b * USE + PRO + NQ * (row - 1))
                        sp.dma_start(qs[:, s, :, :].bitcast(F32), q_dram[:, bass.ds(row * P, P)].rearrange("(t p) n -> p t n", p=P)
                                     ).then_inc(qs_in[s], 16)

                    def load_res(row, s):
                        sp.wait_ge(ot_stored, RB * b + row + 1)
                        sp.dma_start(res[:, s, :, :], res_dram[b, :, bass.ds(row * P, P)].rearrange("(t p) n -> p t n", p=CP)
                                     ).then_inc(res_in[s], 16)

                    def store(row, s):
                        sp.wait_ge(t_free, TR + turn(b, row + 1, -1) + 1)
                        sp.dma_start(out[b, :, bass.ds(row * P, P)].rearrange("(t p) n -> p t n", p=CP),
                                     ot[:, s, :, :]).then_inc(ot_out, 16)
                        sp.wait_ge(ot_out, 16 * (RB * b + row) + 16)
                        sp.sem_inc(ot_stored, 1)

                    for s in range(2):
                        sp.wait_ge(k_in[s], 6 * 16 * NCH // 2 * (b + 1))
                    load_q(0, 0)
                    load_q(1, 1)
                    load_q(2, 0)
                    load_res(0, 0)
                    with sp.Fori(0, RB // 2 - 2) as r:
                        for s in range(2):
                            row = 2 * r + s
                            load_q(row + 3, 1 - s)
                            load_res(row + 1, 1 - s)
                            store(row, s)
                    for row in range(RB - 4, RB):
                        if row + 3 < RB:
                            load_q(row + 3, (row + 3) % 2)
                        if row + 1 < RB:
                            load_res(row + 1, (row + 1) % 2)
                        store(row, row % 2)

                for b in range(B):
                    image(b)

            @block.gpsimd
            def _(pool):
                pool.memset(mhalf[:, :], -0.5).then_inc(powed, 1)
                pool.wait_ge(powed, 1)
                pool.wait_ge(pow_asked, 1)
                pool.tensor_tensor(mix[:, 6:7], mix[:, 5:6], mhalf[:, 0:1], ALU.pow).then_inc(powed, 1)

                for b in range(B):
                    pool.wait_ge(pow_asked, 2 * b + 2)
                    pool.tensor_tensor(gst[:, 3, :], gst[:, 2, :], mhalf[0:CP, 0:CT], ALU.pow).then_inc(powed, 1)
                    pool.wait_ge(g_made, CT * b + CT)
                    for c in range(NCH):
                        cols = slice(c * CH, (c + 1) * CH)
                        pool.tensor_tensor(xg[:, :, cols], xg[:, :, cols], g[:, :, cols], ALU.add).then_inc(xg_made, 1)
                    pool.wait_ge(pow_asked, 2 * b + 3)
                    pool.tensor_tensor(ty[:, :], tv[:, :], mhalf[:, :], ALU.pow).then_inc(powed, 1)
                    for c in range(NCH):
                        pool.wait_ge(xh_made, NCH * b + c + 1)
                        pool.tensor_tensor(xs[:, c % 2, 1, :, :], g[:, :, c * CH:(c + 1) * CH],
                                           xs[:, c % 2, 0, :, :].bitcast(F32), ALU.subtract).then_inc(xl_made, 1)

                    def squares(row):
                        for c in range(NQ):
                            cols = slice(c * QB, (c + 1) * QB)
                            pool.wait_ge(relued, NQ * (RB * b + row) + c + 1)
                            pool.tensor_tensor(rn[:, cols], rn[:, cols], rn[:, cols], ALU.mult).then_inc(squared, 1)

                    with pool.Fori(0, RB) as row:
                        squares(row)

            @block.scalar
            def _(act):
                act.wait_ge(const_in, 16 * NCONST)
                act.activation(mix[:, 0:2], mixw[:, :], ACT.Exp).then_inc(mix_exp, 1)

                for b in range(B):
                    for c in range(NCH):
                        act.wait_ge(dev_made, NCH * b + c + 1)
                        if c >= 2:
                            act.wait_ge(s_full, b * USE + 16 + c - 1)
                        act.activation(sq_buf[:, c % 2, :, :], g[:, :, c * CH:(c + 1) * CH], ACT.Square).then_inc(sq_made, 1)

                    def high_x(c):
                        act.wait_ge(ln_op, LN * b + 4 * c + 4)
                        if c >= 2:
                            act.wait_ge(k_in[c % 2], 6 * 16 * (NCH // 2 * b + c // 2))
                        act.activation(xs[:, c % 2, 0, :, :], g[:, :, c * CH:(c + 1) * CH], ACT.Copy).then_inc(xh_made, 1)

                    def high_qv(c):
                        u = 24 + 2 * c
                        act.wait_ge(s_full, b * USE + u + 1)
                        if c >= 2:
                            act.wait_ge(q_out[c % 2], 4 * 16 * (NCH // 2 * b + c // 2))
                        act.activation(qst[:, c % 2, 0, :, :], ps_s[0:CP, u % 2, :].rearrange("p (t n) -> p t n", t=CT),
                                       ACT.Copy).then_inc(ph_made, 1)
                        u += 1
                        act.wait_ge(s_full, b * USE + u + 1)
                        act.activation(v_hi[:, 4 * c:4 * c + 4, :], ps_s[:, u % 2, :].rearrange("p (m d) -> p m d", m=4)[:, :, 0:C],
                                       ACT.Copy).then_inc(ph_made, 1)

                    for c in range(NCH):
                        high_x(c)
                        if c:
                            high_qv(c - 1)
                    high_qv(NCH - 1)

                    def relu(row, c, first=False):
                        cols = slice(c * QB, (c + 1) * QB)
                        act.wait_ge(s_free, b * USE + 2 + PRO + NQ * row + c + 1)
                        if not first:
                            act.wait_ge(p_made, NQ * (RB * b + row - 1) + c + 1)
                        act.activation(rn[:, cols], vb[:, cols], ACT.Relu).then_inc(relued, 1)

                    def high_group(row, j):
                        act.wait_ge(t_full, turn(b, row, j) + 1)
                        act.wait_ge(w_done, NG * (RB * b + row) + j + 1)
                        act.activation(at_hi[:, j % 4, :], ps_t[:, (j + 1) % TR, :], ACT.Copy).then_inc(hi_made, 1)

                    def exp_piece(row, s, c):
                        if c == 0:
                            act.wait_ge(mx_op, 2 * (RB * b + row) + 2)
                        act.activation(prob[s][:, c * QB:(c + 1) * QB], vb[:, c * QB:(c + 1) * QB], ACT.Exp,
                                       bias=nbias[:, s:s + 1], scale=mix[:, 6:7],
                                       accum_out=sums[:, s, c:c + 1]).then_inc(exped, 1)

                    for c in range(NQ):
                        relu(0, c, True)
                    for c in range(NQ):
                        exp_piece(0, 0, c)

                    def rows(row, s, last):
                        if not last:
                            for c in range(NQ - 1):
                                relu(row + 1, c)
                        for j in range(NG):
                            high_group(row, j)
                            if j == 1 and not last:
                                relu(row + 1, NQ - 1)
                            if 2 <= j < 2 + NQ and not last:
                                exp_piece(row + 1, 1 - s, j - 2)

                    with act.Fori(0, RB // 2 - 1) as r:
                        rows(2 * r, 0, False)
                        rows(2 * r + 1, 1, False)
                    rows(RB - 2, 0, False)
                    rows(RB - 1, 1, True)

            @block.tensor
            def _(pe):
                pe.wait_ge(const_in, 16 * NCONST)
                pe.sem_inc(w_done, 4)
                pe.sem_inc(t_full, 1)
                for o in range(CT):
                    for t in range(CT):
                        ins = pe.matmul(ps_o[0:CP, o * C:(o + 1) * C], wq[:, t, o * CP:(o + 1) * CP], wk[:, t, :],
                                        start=(t == 0), stop=(t == CT - 1))
                ins.then_inc(f_full, 1)

                for b in range(B):
                    n = [0]

                    def pair_free():
                        n[0] += 1
                        pe.wait_ge(s_free, b * USE + n[0])
                        return (n[0] - 1) % 2

                    for c in range(NCH):
                        s = c % 4
                        pe.wait_ge(chunk_in[s], 32 * (2 * b + c // 4 + 1))
                        i = pair_free()
                        for o in range(CT):
                            for t in range(CT):
                                ins = pe.matmul(ps_s[0:CP, i, o * CH:(o + 1) * CH], wp[:, t, o * CP:(o + 1) * CP],
                                                o_buf[:, s, t, :], start=(t == 0), stop=(t == CT - 1))
                        ins.then_inc(s_full, 1)
                    pe.wait_ge(wqk_set, 1)
                    for j, src in enumerate((0, 2)):
                        pe.wait_ge(stat, (STAT + NCH) * b + NCH + (2 if j == 0 else 6))
                        pe.matmul(ps_o[0:CP, j * 8:j * 8 + CT], group[:, :], gst[:, src, :], start=True, stop=True).then_inc(f_full, 1)
                    pe.wait_ge(g_made, CT * b + CT)
                    for c in range(NCH):
                        i = pair_free()
                        for t in range(CT):
                            ins = pe.matmul(ps_s[0:CP, i, 0:CH], meanm[:, :], g[:, t, c * CH:(c + 1) * CH],
                                            start=(t == 0), stop=(t == CT - 1))
                        ins.then_inc(s_full, 1)
                    for c in range(NCH):
                        pe.wait_ge(sq_made, NCH * b + c + 1)
                        i = pair_free()
                        for t in range(CT):
                            ins = pe.matmul(ps_s[0:CP, i, 0:CH], meanm[:, :], sq_buf[:, c % 2, t, :],
                                            start=(t == 0), stop=(t == CT - 1))
                        ins.then_inc(s_full, 1)
                    for c in range(NCH):
                        pe.wait_ge(ln_op, LN * b + 4 * c + 4)
                        i = pair_free()
                        for o in range(CT):
                            for t in range(CT):
                                ins = pe.matmul(ps_s[0:CP, i, o * CH:(o + 1) * CH], wqk[:, t, o * CP:(o + 1) * CP],
                                                g[:, t, c * CH:(c + 1) * CH], start=(t == 0), stop=(t == CT - 1))
                        ins.then_inc(s_full, 1)
                        i = pair_free()
                        for m in range(4):
                            for t in range(CT):
                                ins = pe.matmul(ps_s[:, i, m * 256:m * 256 + C], g[:, t, (4 * c + m) * P:(4 * c + m + 1) * P],
                                                wv[:, t, :], start=(t == 0), stop=(t == CT - 1))
                        ins.then_inc(s_full, 1)

                    def scores(row, s, j):
                        pe.wait_ge(qs_in[s], 16 * (RB // 2 * b + j + 1))
                        for c in range(NQ):
                            pe.wait_ge(s_free, b * USE + PRO + NQ * row + c + 1)
                            for h in range(2):
                                cols = slice(c * QB + h * CH, c * QB + (h + 1) * CH)
                                terms = [(0, 0), (3, 0), (1, 1), (4, 1), (2, 2)]
                                for t, (qt, ktile) in enumerate(terms):
                                    ins = pe.matmul(ps_s[:, c % 2, h * CH:(h + 1) * CH], qs[:, s, qt, :], kst[:, ktile, cols],
                                                    start=(t == 0), stop=(t == len(terms) - 1))
                            ins.then_inc(s_full, 1)

                    def transpose_group(row, s, j):
                        pe.wait_ge(t_free, turn(b, row, j) + 1)
                        if j % 2 == 0:
                            pe.wait_ge(p_made, NQ * (RB * b + row) + j // 2 + 1)
                        for m in range(GR):
                            cols = slice((j * GR + m) * P, (j * GR + m + 1) * P)
                            ins = pe.transpose(ps_t[:, (j + 1) % TR, m * P:(m + 1) * P], prob[s][:, cols], ident[:, :])
                        ins.then_inc(t_full, 1)

                    def weigh_group(row, j):
                        pe.wait_ge(t_free, TR + turn(b, row, j) + 1)
                        if j == 0:
                            pe.wait_ge(ob_made, RB * b + row + 1)
                        for m in range(GR):
                            kt = j * GR + m
                            for t, (a, vp) in enumerate(((at_hi, v_hi), (at_hi, v_lo), (at_lo, v_hi))):
                                ins = pe.matmul(ps_o[:, 0:C], a[:, j % 4, m * P:(m + 1) * P], vp[:, kt, :],
                                                start=(kt == 0 and t == 0), stop=(kt == KT - 1 and t == 2))
                        ins.then_inc(w_done, 1)

                    def weigh(row, s):
                        for j in range(TR):
                            transpose_group(row, s, j)
                        for j in range(NG):
                            weigh_group(row, j)
                            if j + TR < NG:
                                transpose_group(row, s, j + TR)

                    def turn_output(row):
                        pe.wait_ge(ob_made, RB * b + row + 2)
                        pe.wait_ge(t_free, turn(b, row + 1, -1) + 1)
                        for t in range(CT):
                            ins = pe.transpose(ps_t[0:CP, 0, t * P:(t + 1) * P], ob[:, t * CP:(t + 1) * CP], ident[:, :])
                        ins.then_inc(t_full, 1)

                    for s in range(2):
                        pe.wait_ge(k_in[s], 6 * 16 * NCH // 2 * (b + 1))
                    scores(0, 0, 0)
                    scores(1, 1, 0)
                    weigh(0, 0)
                    with pe.Fori(0, RB // 2 - 1) as r:
                        scores(2 * r + 2, 0, r + 1)
                        turn_output(2 * r)
                        weigh(2 * r + 1, 1)
                        scores(2 * r + 3, 1, r + 1)
                        turn_output(2 * r + 1)
                        weigh(2 * r + 2, 0)
                    turn_output(RB - 2)
                    weigh(RB - 1, 1)
                    turn_output(RB - 1)

            @block.vector
            def _(dve):
                dve.sem_inc(s_free, 2)
                dve.sem_inc(ob_made, 1)
                dve.sem_inc(t_free, TR + 1)
                dve.wait_ge(const_in, 16 * NCONST)
                m = [0]

                def mix_step(ins):
                    m[0] += 1
                    ins.then_inc(mix_op, 1)
                    dve.wait_ge(mix_op, m[0])

                dve.wait_ge(mix_exp, 1)
                mix_step(dve.tensor_tensor(mix[:, 2:3], mix[:, 0:1], mix[:, 1:2], ALU.add))
                mix_step(dve.reciprocal(mix[:, 3:4], mix[:, 2:3]))
                mix_step(dve.tensor_scalar(mix[:, 4:6], mix[:, 0:2], mix[:, 3:4], None, ALU.mult))
                dve.tensor_scalar(mix[:, 5:6], mix[:, 5:6], 1e-30, None, ALU.max).then_inc(pow_asked, 1)
                dve.wait_ge(pow_asked, 1)
                dve.wait_ge(powed, 2)
                mix_step(dve.scalar_tensor_tensor(out=mtmp[:, 0:1], in0=mix[:, 5:6], scalar=-0.5, in1=mix[:, 6:7], op0=ALU.mult, op1=ALU.mult))
                mix_step(dve.tensor_tensor(mtmp[:, 1:2], mtmp[:, 0:1], mix[:, 6:7], ALU.mult))
                mix_step(dve.scalar_tensor_tensor(out=mix[:, 6:7], in0=mtmp[:, 1:2], scalar=1.5, in1=mix[:, 6:7], op0=ALU.add, op1=ALU.mult))
                mix_step(dve.tensor_tensor(mix[:, 7:8], mix[:, 5:6], mix[:, 6:7], ALU.mult))
                dve.wait_ge(f_full, 1)
                dve.tensor_scalar(wqk[:, :, :], ps_o[0:CP, 0:CT * C].rearrange("p (t c) -> p t c", t=CT), mix[0:CP, 7:8], None,
                                  ALU.mult).then_inc(wqk_set, 1)

                for b in range(B):
                    n = [0]
                    st = [(STAT + NCH) * b]

                    def full():
                        n[0] += 1
                        dve.wait_ge(s_full, b * USE + n[0])
                        return (n[0] - 1) % 2

                    def stat_step(ins):
                        st[0] += 1
                        ins.then_inc(stat, 1)
                        dve.wait_ge(stat, st[0])

                    for c in range(NCH):
                        s = c % 4
                        cols = slice(c * CH, (c + 1) * CH)
                        i = full()
                        for t in range(CT):
                            ins = dve.scalar_tensor_tensor(out=xg[:, t, cols], in0=ps_s[0:CP, i, t * CH:(t + 1) * CH],
                                                           scalar=pvec[:, t, 0:1], in1=x_buf[:, s, t, :],
                                                           op0=ALU.add, op1=ALU.add)
                        ins.then_inc(s_free, 1)
                        dve.wait_ge(s_free, b * USE + 2 + n[0])
                        for t in range(CT):
                            ins = dve.bn_stats(stats[:, t, c, :], xg[:, t, cols])
                        stat_step(ins)
                    for t in range(CT):
                        ins = dve.bn_aggr(mv[:, t, :], stats[:, t, :, :].rearrange("p c s -> p (c s)"))
                    stat_step(ins)
                    stat_step(dve.tensor_copy(gst[:, 0, :], mv[:, :, 0]))
                    dve.wait_ge(f_full, 1 + FUSE * b + 1)
                    stat_step(dve.tensor_tensor(gst[:, 1, :], gst[:, 0, :], ps_o[0:CP, 0:CT], ALU.subtract))
                    stat_step(dve.tensor_copy(gst[:, 0, :], ps_o[0:CP, 0:CT]))
                    stat_step(dve.tensor_tensor(gst[:, 1, :], gst[:, 1, :], gst[:, 1, :], ALU.mult))
                    stat_step(dve.tensor_tensor(gst[:, 2, :], gst[:, 1, :], mv[:, :, 1], ALU.add))
                    dve.wait_ge(f_full, 1 + FUSE * b + 2)
                    dve.tensor_scalar(gst[:, 2, :], ps_o[0:CP, 8:8 + CT], 1e-5, None, ALU.add).then_inc(pow_asked, 1)
                    dve.wait_ge(pow_asked, 2 * b + 2)
                    dve.wait_ge(powed, 2 * b + 3)
                    stat_step(dve.scalar_tensor_tensor(out=gst[:, 4, :], in0=gst[:, 2, :], scalar=-0.5, in1=gst[:, 3, :],
                                                       op0=ALU.mult, op1=ALU.mult))
                    stat_step(dve.tensor_tensor(gst[:, 4, :], gst[:, 4, :], gst[:, 3, :], ALU.mult))
                    dve.scalar_tensor_tensor(out=gst[:, 3, :], in0=gst[:, 4, :], scalar=1.5, in1=gst[:, 3, :],
                                             op0=ALU.add, op1=ALU.mult).then_inc(g_ready, 1)
                    dve.wait_ge(g_ready, b + 1)
                    for t in range(CT):
                        dve.tensor_scalar(g[:, t, :], xg[:, t, :], gst[:, 0, t:t + 1], gst[:, 3, t:t + 1],
                                          ALU.subtract, ALU.mult).then_inc(g_made, 1)
                    dve.wait_ge(g_made, CT * b + CT)
                    for c in range(NCH):
                        cols = slice(c * CH, (c + 1) * CH)
                        i = full()
                        dve.wait_ge(xg_made, NCH * b + c + 1)
                        for t in range(CT):
                            ins = dve.tensor_tensor(g[:, t, cols], g[:, t, cols], ps_s[0:CP, i, 0:CH], ALU.subtract)
                        ins.then_inc(dev_made, 1)
                        dve.wait_ge(dev_made, NCH * b + c + 1)
                        dve.sem_inc(s_free, 1)
                    for c in range(NCH):
                        i = full()
                        dve.tensor_copy(vb[0:CP, c * CH:(c + 1) * CH], ps_s[0:CP, i, 0:CH]).then_inc(s_free, 1)
                    dve.wait_ge(v_in, 16 * b + 16)
                    if b:
                        dve.wait_ge(r_out, 16 * b)
                    dve.tensor_scalar(tv[:, :], tv[:, :], 1e-5, None, ALU.add).then_inc(pow_asked, 1)
                    dve.wait_ge(pow_asked, 2 * b + 3)
                    dve.wait_ge(powed, 2 * b + 4)
                    dve.scalar_tensor_tensor(out=tt[:, :], in0=tv[:, :], scalar=-0.5, in1=ty[:, :],
                                             op0=ALU.mult, op1=ALU.mult).then_inc(tok, 1)
                    dve.wait_ge(tok, TOK * b + 1)
                    dve.tensor_tensor(tt[:, :], tt[:, :], ty[:, :], ALU.mult).then_inc(tok, 1)
                    dve.wait_ge(tok, TOK * b + 2)
                    dve.scalar_tensor_tensor(out=ty[:, :], in0=tt[:, :], scalar=1.5, in1=ty[:, :],
                                             op0=ALU.add, op1=ALU.mult).then_inc(tok, 2)
                    dve.wait_ge(r_in, 16 * b + 16)

                    def low_qv(c):
                        i = full()
                        dve.wait_ge(ph_made, 2 * (NCH * b + c) + 1)
                        dve.tensor_tensor(qst[:, c % 2, 1, :, :], ps_s[0:CP, i, :].rearrange("p (t n) -> p t n", t=CT),
                                          qst[:, c % 2, 0, :, :].bitcast(F32), ALU.subtract).then_inc(ql_made, 1)
                        dve.wait_ge(ql_made, NCH * b + c + 1)
                        dve.sem_inc(s_free, 1)
                        i = full()
                        dve.wait_ge(ph_made, 2 * (NCH * b + c) + 2)
                        dve.tensor_tensor(v_lo[:, 4 * c:4 * c + 4, :], ps_s[:, i, :].rearrange("p (m d) -> p m d", m=4)[:, :, 0:C],
                                          v_hi[:, 4 * c:4 * c + 4, :].bitcast(F32), ALU.subtract).then_inc(s_free, 1)

                    for c in range(NCH):
                        cols = slice(c * CH, (c + 1) * CH)
                        for t in range(CT):
                            dve.scalar_tensor_tensor(out=g[:, t, cols], in0=g[:, t, cols], scalar=pvec[:, t, 1:2],
                                                     in1=rn[0:CP, cols], op0=ALU.mult, op1=ALU.mult).then_inc(ln_op, 1)
                        for t in range(CT):
                            dve.wait_ge(ln_op, LN * b + 4 * c + 1 + t)
                            dve.tensor_scalar(g[:, t, cols], g[:, t, cols], pvec[:, t, 2:3], None, ALU.add).then_inc(ln_op, 1)
                        if c > 0:
                            low_qv(c - 1)
                    low_qv(NCH - 1)

                    def take_piece(row, s, c):
                        dve.wait_ge(s_full, b * USE + PRO + NQ * row + c + 1)
                        if b or not isinstance(row, int) or row:
                            dve.wait_ge(exped, NQ * (RB * b + row - 1) + c + 1)
                        dve.tensor_scalar(vb[:, c * QB:(c + 1) * QB], ps_s[:, c % 2, :], 1.0, None, ALU.mult, ALU.max,
                                          accum_out=mx[:, s, c:c + 1]).then_inc(s_free, 1)

                    def maximum(row, s):
                        dve.wait_ge(s_free, b * USE + PRO + NQ * row + NQ + 2)
                        dve.tensor_reduce(nbias[:, s:s + 1], mx[:, s, :], AX_X, ALU.max, negate=True).then_inc(mx_op, 1)
                        dve.wait_ge(mx_op, 2 * (RB * b + row) + 1)
                        dve.tensor_scalar(nbias[:, s:s + 1], nbias[:, s:s + 1], mix[:, 6:7], None, ALU.mult).then_inc(mx_op, 1)

                    def coefficient(row, s):
                        at = 3 * (RB * b + row)
                        dve.wait_ge(exped, NQ * (RB * b + row) + NQ)
                        dve.tensor_reduce(coef[:, s:s + 1], sums[:, s, :], AX_X, ALU.add).then_inc(c_op, 1)
                        dve.wait_ge(c_op, at + 1)
                        dve.reciprocal(coef[:, s:s + 1], coef[:, s:s + 1]).then_inc(c_op, 1)
                        dve.wait_ge(c_op, at + 2)
                        dve.tensor_scalar(coef[:, s:s + 1], coef[:, s:s + 1], mix[:, 4:5], None, ALU.mult).then_inc(c_op, 1)
                        dve.wait_ge(c_op, at + 3)

                    def combine(row, s, c):
                        cols = slice(c * QB, (c + 1) * QB)
                        dve.wait_ge(squared, NQ * (RB * b + row) + c + 1)
                        dve.scalar_tensor_tensor(out=prob[s][:, cols], in0=prob[s][:, cols], scalar=coef[:, s:s + 1],
                                                 in1=rn[:, cols], op0=ALU.mult, op1=ALU.add).then_inc(p_made, 1)

                    def low_group(row, j):
                        dve.wait_ge(hi_made, NG * (RB * b + row) + j + 1)
                        dve.tensor_tensor(at_lo[:, j % 4, :], ps_t[:, (j + 1) % TR, :], at_hi[:, j % 4, :].bitcast(F32),
                                          ALU.subtract).then_inc(t_free, 1)

                    def copy_output(row):
                        dve.wait_ge(w_done, 4 + NG * (RB * b + row) + NG)
                        dve.tensor_copy(ob[:, :], ps_o[:, 0:C]).then_inc(ob_made, 1)

                    def add_output(row, s, j):
                        dve.wait_ge(t_full, turn(b, row + 1, -1) + 1)
                        dve.wait_ge(res_in[s], 16 * (RB // 2 * b + j + 1))
                        dve.wait_ge(ot_stored, RB * b + row + 1)
                        dve.tensor_tensor(ot[:, s, :, :], ps_t[0:CP, 0, 0:CT * P].rearrange("p (t n) -> p t n", t=CT),
                                          res[:, s, :, :], ALU.add).then_inc(t_free, 1)

                    def while_scores(row, s, last):
                        for c in range(NQ):
                            if c:
                                combine(row, s, c)
                            if c and not last:
                                take_piece(row + 1, 1 - s, c - 1)
                        if not last:
                            take_piece(row + 1, 1 - s, NQ - 1)
                            maximum(row + 1, 1 - s)

                    def while_products(row, s, last):
                        for j in range(NG):
                            low_group(row, j)
                            if j == 6 and not last:
                                coefficient(row + 1, 1 - s)
                        if not last:
                            combine(row + 1, 1 - s, 0)
                        copy_output(row)

                    for c in range(NQ):
                        take_piece(0, 0, c)
                    maximum(0, 0)
                    coefficient(0, 0)
                    combine(0, 0, 0)
                    while_scores(0, 0, False)
                    while_products(0, 0, False)
                    with dve.Fori(0, RB // 2 - 1) as r:
                        while_scores(2 * r + 1, 1, False)
                        add_output(2 * r, 0, r)
                        while_products(2 * r + 1, 1, False)
                        while_scores(2 * r + 2, 0, False)
                        add_output(2 * r + 1, 1, r)
                        while_products(2 * r + 2, 0, False)
                    while_scores(RB - 1, 1, True)
                    add_output(RB - 2, 0, RB // 2 - 1)
                    while_products(RB - 1, 1, True)
                    add_output(RB - 1, 1, RB // 2 - 1)


TILE_BLOCKS = [(0, 4), (8, 9), (1, 5), (2, 6), (10, 11), (3, 7)]


def build(nc, a, out):
    consts = {k: a[k] for k in ("group", "mean", "ident", "ones_blk", "den_sel")}
    z_dram = nc.dram_tensor("z_scratch", [B, C, N], F32, kind="Internal").ap()
    ss_dram = nc.dram_tensor("ss_scratch", [2, N], F32, kind="Internal").ap()
    rn_dram = nc.dram_tensor("rn_scratch", [2, N], F32, kind="Internal").ap()
    o_dram = nc.dram_tensor("o_scratch", [B * HEADS, HD, N], F32, kind="Internal").ap()
    m_dram = nc.dram_tensor("m_scratch", [1, N], F32, kind="Internal").ap()
    r_dram = nc.dram_tensor("r_scratch", [1, N], F32, kind="Internal").ap()
    res_dram = nc.dram_tensor("res_scratch", [B, C, N], F32, kind="Internal").ap()
    q_dram = nc.dram_tensor("q_scratch", [4 * C, N], F32, kind="Internal").ap()
    group_norm_and_store(nc, a["x"], consts, z_dram)
    layer0(nc, z_dram, a["w_qkv"], a["vecs"], a["temperature"], consts, ss_dram, rn_dram, o_dram)
    o_by_image = o_dram.rearrange("(b h) d n -> b (h d) n", b=B)
    layer1(nc, a["x"], o_by_image, {k: a[k] for k in ("wp", "wq", "wk", "wv", "pvec", "mix")}, consts, m_dram, r_dram,
           res_dram, q_dram, out)


def kernel(x, L0_conv_w_qkv, L0_conv_b_qkv, L0_conv_w_dw, L0_conv_b_dw, L0_conv_w_proj, L0_conv_b_proj,
           L0_conv_temperature, L1_conv_ln_w, L1_conv_ln_b, L1_conv_Wq, L1_conv_Wk, L1_conv_Wv, L1_conv_w1, L1_conv_w2):
    import numpy as np
    import concourse.bacc as bacc
    from concourse.bass_utils import run_bass_kernel_spmd

    order = [block for pair in TILE_BLOCKS for block in pair]

    def by_tile(w):
        t = np.asarray(w).reshape(12, HD, -1)[order].reshape(6, 2, HD, -1)
        return np.concatenate([t, t])

    def transposed(w):
        return np.ascontiguousarray(np.asarray(w).T.reshape(CT, CP, -1).transpose(1, 0, 2))

    def by_output(w):
        return np.asarray(w).reshape(CT, CP, -1).transpose(1, 0, 2)

    def channels(v):
        return np.asarray(v).reshape(CT, CP).T

    w_qkv = by_tile(L0_conv_w_qkv).reshape(12, 2, HD, CT, CP).transpose(0, 4, 3, 1, 2)
    vecs = np.concatenate([by_tile(L0_conv_b_qkv), by_tile(L0_conv_w_dw), by_tile(L0_conv_b_dw)], axis=3)
    temperature = np.asarray(L0_conv_temperature).reshape(1, HEADS)

    f = np.float32
    ch = np.arange(CP)
    rows = np.arange(P)
    block_of = np.where(rows % HALF < HD, rows // HALF, -1)
    inputs = {
        "x": np.asarray(x).reshape(B, C, N),
        "w_qkv": w_qkv,
        "vecs": vecs,
        "temperature": np.concatenate([temperature, temperature], axis=1),
        "wp": transposed(L0_conv_w_proj),
        "wq": by_output(L1_conv_Wq),
        "wk": by_output(L1_conv_Wk),
        "wv": transposed(L1_conv_Wv),
        "pvec": np.stack([channels(L0_conv_b_proj), channels(L1_conv_ln_w), channels(L1_conv_ln_b)], axis=2),
        "mix": np.concatenate([np.asarray(L1_conv_w1), np.asarray(L1_conv_w2)]).reshape(1, 2),
        "group": ((ch[:, None] // 6 == ch[None, :] // 6) / 6.0).astype(f),
        "mean": np.full((CP, CP), 1.0 / C, f),
        "ident": np.eye(P, dtype=f),
        "ones_blk": ((block_of[:, None] == block_of[None, :]) & (block_of[:, None] >= 0)).astype(f),
        "den_sel": (rows[:, None] == (rows[None, :] // HALF) * HALF + HD).astype(f),
    }
    nc = bacc.Bacc("TRN2", target_bir_lowering=False, num_devices=1)
    arrays, aps = {}, {}
    for name, value in inputs.items():
        value = np.ascontiguousarray(value)
        arrays[f"in_{name}"] = value
        aps[name] = nc.dram_tensor(f"in_{name}", value.shape, mybir.dt.from_np(value.dtype), kind="ExternalInput").ap()
    out = nc.dram_tensor("out", [B, C, N], F32, kind="ExternalOutput").ap()
    build(nc, aps, out)
    result = run_bass_kernel_spmd(nc, [arrays], core_ids=[0])
    return result.results[0]["out"].reshape(B, C, HH, WW)
```
